# Optimizing a Trainium2 kernel written in Bass

```python
import numpy as np
import jax
import jax.numpy as jnp

def _softmax(x, axis=-1):
    return jax.nn.softmax(x, axis=axis)

def _gelu(x):
    return jax.nn.gelu(x, approximate=True)

def _silu(x):
    return jax.nn.silu(x)

def _sigmoid(x):
    return jax.nn.sigmoid(x)

def _layernorm(x, axis=-1, eps=1e-05):
    m = jnp.mean(x, axis=axis, keepdims=True)
    v = jnp.var(x, axis=axis, keepdims=True)
    return (x - m) / jnp.sqrt(v + eps)

def _scatter_add(tgt, idx, src, axis=0):
    return tgt.at[idx].add(src)

def _segment_sum(src, seg, n):
    return jax.ops.segment_sum(src, seg, n)
kernel_name = 'mk_adj_ffn_d1_adj_r2_b1c21b'

def setup_inputs(seed: int=0):
    np.random.seed(seed)
    _w = jnp.asarray

    def _rec_inputs():
        import jax
        import jax.numpy as jnp
        _gk = jax.random.key(seed)
        x = -0.0002928 + 1 * jax.random.normal(jax.random.fold_in(_gk, 1), (2048, 512), jnp.float32)
        _a = jax.random.bernoulli(jax.random.fold_in(_gk, 2), 0.0078125, (2048, 2048))
        _a = jnp.logical_or(_a, jnp.swapaxes(_a, -1, -2))
        _a = jnp.logical_or(_a, jnp.eye(2048, dtype=bool))
        _af = _a.astype(jnp.float32)
        adj = _af
        return (x, adj)
    x, adj = _rec_inputs()

    def _L0_gnn_setup():
        import jax, jax.numpy as jnp
        import numpy as np
        N = 2048
        D_IN = 512
        H = 16
        DH = D_IN // H
        ALPHA = 0.2
        MASK_VAL = -65500.0
        key = jax.random.key(seed)
        ks = jax.random.split(key, 7)
        x = jax.random.normal(ks[0], (N, D_IN), dtype=jnp.float32)
        adj = jax.random.randint(ks[1], (N, N), 0, 2).astype(jnp.float32)
        s = 1.0 / np.sqrt(D_IN)
        W_seq = jax.random.normal(ks[2], (D_IN, D_IN), dtype=jnp.float32) * s
        a1 = jax.random.normal(ks[3], (DH,), dtype=jnp.float32) / np.sqrt(DH)
        a2 = jax.random.normal(ks[4], (DH,), dtype=jnp.float32) / np.sqrt(DH)
        W_out = jax.random.normal(ks[5], (D_IN, D_IN), dtype=jnp.float32) * s
        b_out = jax.random.normal(ks[6], (D_IN,), dtype=jnp.float32) * 0.01
        return {'x': x, 'adj': adj, 'W_seq': W_seq, 'a1': a1, 'a2': a2, 'W_out': W_out, 'b_out': b_out}
    _L0_gnn_all = _L0_gnn_setup()
    _L0_gnn_in = {k: v for k, v in _L0_gnn_all.items() if k in ('W_seq', 'a1', 'a2', 'W_out', 'b_out')}
    del _L0_gnn_all

    def _L0_ffn_setup():
        import jax, jax.numpy as jnp
        import numpy as np
        MICRO_BATCHES = 2
        TOP_K = 2
        LN_EPS = 1e-05
        B, S, D = (4, 2048, 512)
        E = 8
        DFF = 4 * D

        def _layernorm(x, g, b):
            mu = jnp.mean(x, axis=-1, keepdims=True)
            var = jnp.mean(jnp.square(x - mu), axis=-1, keepdims=True)
            return (x - mu) * jax.lax.rsqrt(var + LN_EPS) * g + b
        key = jax.random.key(seed)
        ks = jax.random.split(key, 12)
        sd = 1.0 / np.sqrt(D)
        sf = 1.0 / np.sqrt(DFF)
        return {'x': jax.random.normal(ks[0], (B, S, D), dtype=jnp.float32), 'ln_g': jnp.ones((D,), jnp.float32), 'ln_b': jnp.zeros((D,), jnp.float32), 'attn_w': jax.random.normal(ks[1], (D, D), jnp.float32) * sd, 'attn_b': jnp.zeros((D,), jnp.float32), 'gate_w': jax.random.normal(ks[2], (D, E), jnp.float32) * sd, 'w1': jax.random.normal(ks[3], (E, D, DFF), jnp.float32) * sd, 'b1': jnp.zeros((E, DFF), jnp.float32), 'w2': jax.random.normal(ks[4], (E, DFF, D), jnp.float32) * sf, 'b2': jnp.zeros((E, D), jnp.float32), 'next_w': jax.random.normal(ks[5], (D, D), jnp.float32) * sd, 'next_b': jnp.zeros((D,), jnp.float32)}
    _L0_ffn_all = _L0_ffn_setup()
    _L0_ffn_in = {k: v for k, v in _L0_ffn_all.items() if k in ('ln_g', 'ln_b', 'attn_w', 'attn_b', 'gate_w', 'w1', 'b1', 'w2', 'b2', 'next_w', 'next_b')}
    del _L0_ffn_all
    return {'x': x, 'adj': adj, 'L0_gnn_W_seq': _L0_gnn_in['W_seq'], 'L0_gnn_a1': _L0_gnn_in['a1'], 'L0_gnn_a2': _L0_gnn_in['a2'], 'L0_gnn_W_out': _L0_gnn_in['W_out'], 'L0_gnn_b_out': _L0_gnn_in['b_out'], 'L0_ffn_ln_g': _L0_ffn_in['ln_g'], 'L0_ffn_ln_b': _L0_ffn_in['ln_b'], 'L0_ffn_attn_w': _L0_ffn_in['attn_w'], 'L0_ffn_attn_b': _L0_ffn_in['attn_b'], 'L0_ffn_gate_w': _L0_ffn_in['gate_w'], 'L0_ffn_w1': _L0_ffn_in['w1'], 'L0_ffn_b1': _L0_ffn_in['b1'], 'L0_ffn_w2': _L0_ffn_in['w2'], 'L0_ffn_b2': _L0_ffn_in['b2'], 'L0_ffn_next_w': _L0_ffn_in['next_w'], 'L0_ffn_next_b': _L0_ffn_in['next_b']}

def reference(x, adj, L0_gnn_W_seq, L0_gnn_a1, L0_gnn_a2, L0_gnn_W_out, L0_gnn_b_out, L0_ffn_ln_g, L0_ffn_ln_b, L0_ffn_attn_w, L0_ffn_attn_b, L0_ffn_gate_w, L0_ffn_w1, L0_ffn_b1, L0_ffn_w2, L0_ffn_b2, L0_ffn_next_w, L0_ffn_next_b):
    import jax
    import jax.numpy as jnp

    def _L0_gnn_ref(x, adj, W_seq, a1, a2, W_out, b_out):
        import jax, jax.numpy as jnp
        import numpy as np
        N = 2048
        D_IN = 512
        H = 16
        DH = D_IN // H
        ALPHA = 0.2
        MASK_VAL = -65500.0
        seq = (x @ W_seq).reshape(N, H, DH)
        score1 = jnp.einsum('nhd,d->hn', seq, a1)
        score2 = jnp.einsum('nhd,d->hn', seq, a2)
        scores = score1[:, :, None] + score2[:, None, :]
        scores = jax.nn.leaky_relu(scores, negative_slope=ALPHA)
        scores = scores + (1.0 - adj)[None, :, :] * MASK_VAL
        attn = jax.nn.softmax(scores, axis=-1)
        hidden = jnp.einsum('hij,jhd->ihd', attn, seq).reshape(N, D_IN)
        hidden = hidden @ W_out + b_out
        return jax.nn.elu(hidden)

    def _L0_ffn_ref(x, ln_g, ln_b, attn_w, attn_b, gate_w, w1, b1, w2, b2, next_w, next_b):
        import jax, jax.numpy as jnp
        import numpy as np
        MICRO_BATCHES = 2
        TOP_K = 2
        LN_EPS = 1e-05
        B, S, D = (4, 2048, 512)
        E = 8
        DFF = 4 * D

        def _layernorm(x, g, b):
            mu = jnp.mean(x, axis=-1, keepdims=True)
            var = jnp.mean(jnp.square(x - mu), axis=-1, keepdims=True)
            return (x - mu) * jax.lax.rsqrt(var + LN_EPS) * g + b
        Bx, Sx, Dx = x.shape
        N = Bx * Sx
        x_flat = x.reshape(N, Dx)
        x_attn = _layernorm(x_flat, ln_g, ln_b) @ attn_w + attn_b + x_flat
        logits = x_attn @ gate_w
        _ = jax.lax.top_k(logits, TOP_K)
        tpe = N // (MICRO_BATCHES * E)
        g = x_attn.reshape(MICRO_BATCHES, E, tpe, Dx)
        h = jax.nn.gelu(jnp.einsum('metd,edf->metf', g, w1) + b1[None, :, None, :], approximate=False)
        y = jnp.einsum('metf,efd->metd', h, w2) + b2[None, :, None, :]
        out = jax.nn.gelu(y @ next_w + next_b, approximate=False)
        return out.reshape(Bx, Sx, Dx)
    x = x + _L0_gnn_ref(_layernorm(x, axis=-1), adj, L0_gnn_W_seq, L0_gnn_a1, L0_gnn_a2, L0_gnn_W_out, L0_gnn_b_out)
    x = x + _L0_ffn_ref(_layernorm(x, axis=-1)[None], L0_ffn_ln_g, L0_ffn_ln_b, L0_ffn_attn_w, L0_ffn_attn_b, L0_ffn_gate_w, L0_ffn_w1, L0_ffn_b1, L0_ffn_w2, L0_ffn_b2, L0_ffn_next_w, L0_ffn_next_b)[0]
    return x

_drawn_inputs = setup_inputs


def setup_inputs(seed=0):
    import zlib

    import numpy as np

    out = dict(_drawn_inputs(seed))
    spreads = {'L0_ffn_ln_g': (1.0, 0.2),
     'L0_ffn_ln_b': (0.0, 0.1),
     'L0_ffn_attn_b': (0.0, 0.1),
     'L0_ffn_b1': (0.0, 0.1),
     'L0_ffn_b2': (0.0, 0.1),
     'L0_ffn_next_b': (0.0, 0.1)}
    factors = {'L0_gnn_b_out': 6.052}
    for name, (base, spread) in spreads.items():
        noise = np.random.default_rng([zlib.crc32(name.encode()), seed]).standard_normal(out[name].shape)
        drawn = base * np.exp(spread * noise) if base else spread * noise
        out[name] = jnp.asarray(drawn.astype(out[name].dtype))
    for name, factor in factors.items():
        out[name] = (out[name] * factor).astype(out[name].dtype)
    return out
```

```python
from contextlib import ExitStack

import concourse.bass as bass
from concourse import mybir

F32 = mybir.dt.float32
F16 = mybir.dt.float16
BF16 = mybir.dt.bfloat16
F8 = mybir.dt.float8e4
U8 = mybir.dt.uint8
U32 = mybir.dt.uint32
ALU = mybir.AluOpType
ACT = mybir.ActivationFunctionType
AX = mybir.AxisListType

P = 128
N = 2048
D = 512
H = 16
DH = D // H
V1 = DH + 1
T = N // P
K = D // P
E = 8
F = 2048
FT = F // P
HALF = N // 2
PAIRS = H // 2
VEC = E * K + 2 * K
EPS = 1e-5

WS = 2.0 ** 10
XS = 2.0 ** 8
HS = 2.0 ** 6
KAPPA = 2.0 ** 10
BIG = 2.0 ** 100
NEG1 = 184.0
POS1 = 56.0

DVE_CMP = {(0, 1), (1, 1), (2, 1)}


def gat_moe_kernel(nc, x, adj, w_seq, a1, a2, w_out, b_out, ln_g, ln_b, attn_w, attn_b, w1, b1,
                   w2, b2, next_w, next_b, out):
    ctx = ExitStack()
    with ctx:
        def sb(name, shape, dt):
            return ctx.enter_context(nc.sbuf_tensor(name, shape, dt))

        def sem(name):
            return ctx.enter_context(nc.semaphore(name))

        def view(region, start, dt, *dims):
            size = {F32: 4, F16: 2, BF16: 2, F8: 1, U8: 1, U32: 4}[dt]
            n = size
            for d in dims:
                n *= d
            ap = region[:, start:start + n].bitcast(dt)
            names = [f"d{i}" for i in range(len(dims))]
            if len(dims) > 1:
                ap = ap.rearrange(f"p ({' '.join(names)}) -> p {' '.join(names)}",
                                  **dict(zip(names[1:], dims[1:])))
            return ap

        region_g = sb("region_g", [P, 65536], U8)
        region_m = sb("region_m", [P, 32768], U8)
        region_s = sb("region_s", [P, T * H * V1 * 4], U8)
        region_w = sb("region_w", [P, 3 * 8192], U8)
        region_x = sb("region_x", [P, 37504], U8)
        region_e = sb("region_e", [P, 8448], U8)
        region_c = sb("region_c", [P, 6144], U8)

        x_all = view(region_g, 0, F32, T, D)
        adj_f = [view(region_g, 32768 + 8192 * u, F32, N) for u in range(2)]
        adj_b = [view(region_g, 49152 + 4096 * u, BF16, N) for u in range(2)]
        wseq_hi = view(region_g, 57344, F16, K, D)
        wseq_lo = view(region_g, 61440, F16, K, D)
        wa_prod = view(region_m, 0, F32, K * H, DH)
        b1_rows = view(region_m, 8192, F32, P)
        vec_rows = view(region_m, 8704, F32, P)
        mask_u8 = view(region_m, 0, U8, T, N)
        mask_f8 = view(region_m, 0, F8, T, N)
        mask_u32 = view(region_m, 0, U32, T, N // 4)
        wseq_f = view(region_x, 0, F32, K, D)
        wother_f = view(region_x, 8192, F32, K * D)
        xn0 = [view(region_x, 16384 + 2048 * u, F32, D) for u in range(2)]
        xnT_hi = [view(region_x, 20480 + 2048 * u, F16, K, P) for u in range(2)]
        xnT_lo = [view(region_x, 21504 + 2048 * u, F16, K, P) for u in range(2)]
        s1T = view(region_x, 24832, F32, N)
        wa_f = view(region_x, 33280, F32, K, 2, H)
        wa_hi = view(region_x, 33792, F16, K, 2 * H)
        wa_lo = view(region_x, 34048, F16, K, 2 * H)
        a_row = view(region_x, 34304, F32, 2, DH)
        s12 = view(region_e, 0, F32, T, 2 * H)
        su = view(region_e, 2048, F32, T, H)
        st_a = view(region_e, 3072, F32, T, H)
        st_c = view(region_e, 4096, F32, T, H)

        g_u8 = [view(region_g, 32768 * b, U8, T, 2, HALF) for b in range(2)]
        g_f8 = [view(region_g, 32768 * b, F8, T, 2, HALF) for b in range(2)]
        g_u32 = [view(region_g, 32768 * b, U32, T, 2, HALF // 4) for b in range(2)]
        seqv = view(region_s, 0, F32, T, H * V1)
        s1_row = [view(region_x, 8192 * b, F32, 2, HALF) for b in range(2)]
        w_att = [view(region_x, 16384 + 8448 * b, F16, T, 2, 4 * V1) for b in range(2)]
        w_prod = view(region_x, 33280, F32, T // 2, 2, 2 * V1)
        acc_lo = [view(region_e, 2112 * g, F32, 4, 2, 2 * V1) for g in range(2)]
        acc_s = [view(region_e, 4224 + 2112 * g, F32, 4, 2, 2 * V1) for g in range(2)]
        thr = view(region_c, 0, F32, PAIRS, 2, T, 2)
        e_b = view(region_c, 2048, F32, T, H)
        e_d = view(region_c, 3072, F32, T, H)
        a_c = view(region_c, 4096, F32, T, H, 2)
        thr_now = [sb(f"thr_now{b}", [P, 2, T, 2], F32) for b in range(2)]

        wpart_hi = [view(region_g, 8192 * c, F16, 4, D) for c in range(8)]
        wpart_lo = [view(region_g, 8192 * c + 4096, F16, 4, D) for c in range(8)]
        h_hi = view(region_m, 0, F16, FT, 256)
        h_lo = view(region_m, 8192, F16, FT, 256)
        parts = [(view(region_m, 16384 + 4096 * i, F16, K, 256),
                  view(region_m, 18432 + 4096 * i, F16, K, 256)) for i in range(4)]
        (hidT_hi, hidT_lo), (xlT_hi, xlT_lo), (xaT_hi, xaT_lo), (yT_hi, yT_lo) = parts
        w_stage = [view(region_x, 8192 * s, F32, 4, D) for s in range(2)]
        hid = view(region_x, 16384, F32, 2, D)
        xl = view(region_x, 20480, F32, K, 256)
        x_res = view(region_x, 20480, F32, 2, D)
        xn = view(region_x, 24576, F32, 2, D)
        h_f = [view(region_x, 28672 + 2048 * i, F32, 2, 256) for i in range(2)]
        y_f = view(region_x, 32768, F32, K, 256)
        y_rows = view(region_x, 32768, F32, 2, D)
        z = view(region_e, 0, F32, 2, D)
        en = view(region_e, 4096, F32, 2, D)
        bout_row, battn_row, bnext_row = [view(region_c, 2048 * i, F32, D) for i in range(3)]
        fixed = [(view(region_w, 8192 * i, F16, K, D), view(region_w, 8192 * i + 4096, F16, K, D))
                 for i in range(3)]
        (wout_hi, wout_lo), (wattn_hi, wattn_lo), (wnext_hi, wnext_lo) = fixed

        ident = sb("ident", [P, P], F32)
        ident_b = sb("ident_b", [P, P], BF16)
        s1_now = [sb(f"s1_now{u}", [P, H], F32) for u in range(2)]
        stats = sb("stats", [P, T, 6], F32)
        mv = sb("mv", [P, T, 2], F32)
        ln_v = sb("ln_v", [P, T], F32)
        ln_s = sb("ln_s", [P, T], F32)
        ln_t = sb("ln_t", [P, T], F32)
        ln_r = sb("ln_r", [P, T], F32)
        rowsum = sb("rowsum", [P, 2], F32)
        lonely = sb("lonely", [P, 2], F32)
        smax = sb("smax", [P, H], F32)
        smax_all = sb("smax_all", [P, H], F32)
        rden = sb("rden", [P, 2, H], F32)
        b1_col = sb("b1_col", [P, E, FT], F32)
        vec_col = sb("vec_col", [P, VEC], F32)
        b2_col = vec_col[:, 0:E * K].rearrange("p (e k) -> p e k", k=K)
        g_col, b_col = vec_col[:, E * K:E * K + K], vec_col[:, E * K + K:VEC]

        s1T_dram = nc.dram_tensor("s1T_dram", (H, N), F32, kind="Internal").ap()

        ps = ctx.enter_context(nc.psum_tensor("ps", [P, 8, 512], F32))
        ps_adjT = [ps[:, 6 + i, :].bitcast(BF16).rearrange("p (j i) -> p j i", i=P) for i in range(2)]
        ps_tr = ps[:, 0:2, :].rearrange("p b c -> p (b c)").rearrange("p (k c) -> p k c", k=K)
        ps_mm = ps[:, 2:4, :]
        ps_h = [ps[:, 4 + i, :].rearrange("p (f c) -> p f c", f=2) for i in range(2)]
        ps_y = ps[:, 6:8, :].rearrange("p b c -> p (b c)").rearrange("p (k c) -> p k c", k=K)

        x_t = x.rearrange("(t p) d -> p t d", p=P)
        x_e = x.rearrange("(u t p) d -> p u t d", p=P, u=2)
        out_e = out.rearrange("(u t p) d -> p u t d", p=P, u=2)
        adj_t = adj.rearrange("(t p) j -> p t j", p=P)
        w1_c = w1.rearrange("e (k p) (c f) -> p e c k f", p=P, c=4)
        w2_c = w2.rearrange("e (c k p) d -> p e c k d", p=P, c=4)

        x_in = [sem(f"x_in{i}") for i in range(4)]
        wseq_in, a_in, wother_in, cols_in = sem("wseq_in"), sem("a_in"), sem("wother_in"), sem("cols_in")
        adj_in = [sem(f"adj_in{u}") for u in range(2)]
        ident_made, cols_turned, cols_evac = sem("ident_made"), sem("cols_turned"), sem("cols_evac")
        wseq_hi_done, wseq_lo_done, wa_step = sem("wseq_hi_done"), sem("wseq_lo_done"), sem("wa_step")
        wother_step = sem("wother_step")
        ln_step, sqrt_done = sem("ln_step"), sem("sqrt_done")
        xn_ready, xT_done, xhi_done, xlo_done = sem("xn_ready"), sem("xT_done"), sem("xhi_done"), sem("xlo_done")
        s_done, seq_done, s_evac, seq_evac = sem("s_done"), sem("seq_done"), sem("s_evac"), sem("seq_evac")
        adj_cast, lonely_done, adj_bin = sem("adj_cast"), sem("lonely_done"), sem("adj_bin")
        adjT_a, adjT_b, mask_dve, mask_act = sem("adjT_a"), sem("adjT_b"), sem("mask_dve"), sem("mask_act")
        sT_done, sT_evac, s1T_out = sem("sT_done"), sem("sT_evac"), sem("s1T_out")
        smax_done, smax_all_done = sem("smax_done"), sem("smax_all_done")
        coef_step, exp_done = sem("coef_step"), sem("exp_done")
        s1_row_in = [sem(f"s1_row_in{b}") for b in range(2)]
        thr_ready, w_prod_step, w_ready = sem("thr_ready"), sem("w_prod_step"), sem("w_ready")
        act_cmp, dve_cmp, g_ready, g_free = sem("act_cmp"), sem("dve_cmp"), sem("g_ready"), sem("g_free")
        acc_done, lo_copied, acc_free = sem("acc_done"), sem("lo_copied"), sem("acc_free")
        acc_scaled, num_done = sem("acc_scaled"), sem("num_done")
        rows_in = sem("rows_in")
        w_in = [sem(f"w_in{s}") for s in range(2)]
        whi_done, wlo_done = sem("whi_done"), sem("wlo_done")
        rden_done, hid_ready, x_res_in = sem("rden_done"), sem("hid_ready"), sem("x_res_in")
        tr_done, tr_hi, tr_free = sem("tr_done"), sem("tr_hi"), sem("tr_free")
        mo_done, mo_free, ma_done, ma_free = sem("mo_done"), sem("mo_free"), sem("ma_done"), sem("ma_free")
        nx_done, nx_free = sem("nx_done"), sem("nx_free")
        neg_ready, en_ready, elu_step = sem("neg_ready"), sem("en_ready"), sem("elu_step")
        norm_step, norm_sqrt, xh_ready = sem("norm_step"), sem("norm_sqrt"), sem("xh_ready")
        xl_hi_done, xl_lo_done, xa_ready = sem("xl_hi_done"), sem("xl_lo_done"), sem("xa_ready")
        h_done, h_gelu, hhi_done, hlo_done = sem("h_done"), sem("h_gelu"), sem("hhi_done"), sem("hlo_done")
        y_done, y_free, yhi_done, ylo_done = sem("y_done"), sem("y_free"), sem("yhi_done"), sem("ylo_done")
        og_ready, out_ready, out_stored = sem("og_ready"), sem("out_ready"), sem("out_stored")

        def settle(eng):
            eng.nop(nofuse=True)

        block = ctx.enter_context(nc.Block())

        @block.sync
        def _(sp):
            for i in range(4):
                if i == 1:
                    sp.dma_start(wseq_f, w_seq.rearrange("(k p) n -> p k n", p=P)).then_inc(wseq_in, 16)
                    sp.dma_start(a_row[:, 0, :], a1.partition_broadcast(P)).then_inc(a_in, 16)
                    sp.dma_start(a_row[:, 1, :], a2.partition_broadcast(P)).then_inc(a_in, 16)
                sp.dma_start(x_all[:, 4 * i:4 * i + 4, :], x_t[:, 4 * i:4 * i + 4, :]).then_inc(x_in[i], 16)
            for u in range(2):
                sp.dma_start(adj_f[u], adj_t[:, u, :]).then_inc(adj_in[u], 16)
            with sp.Fori(1, T // 2) as i:
                for u in range(2):
                    sp.wait_ge(adj_cast, 2 * i + u - 1)
                    sp.dma_start(adj_f[u], adj_t[:, 2 * i + u, :]).then_inc(adj_in[u], 16)

            def load_s1_row(q, b):
                sp.dma_start(s1_row[b], s1T_dram[bass.ds(2 * q, 2), b * HALF:(b + 1) * HALF]
                             .partition_broadcast(P)).then_inc(s1_row_in[b], 16)

            sp.wait_ge(s1T_out, 16)
            sp.wait_ge(wother_step, 9)
            for b in range(2):
                load_s1_row(0, b)
            with sp.Fori(1, PAIRS) as q:
                for b in range(2):
                    sp.wait_ge(act_cmp, 16 * q + 8 * b - 8)
                    sp.wait_ge(dve_cmp, 16 * q + 8 * b - 8)
                    load_s1_row(q, b)

            sp.wait_ge(act_cmp, 16 * PAIRS)
            sp.wait_ge(dve_cmp, 16 * PAIRS)

            def load_chunk(e, c, first=False):
                if not first:
                    sp.wait_ge(wlo_done, 8 * e + c - 1)
                src = w1_c[:, e, c] if c < 4 else w2_c[:, e, c - 4]
                sp.dma_start(w_stage[c % 2], src).then_inc(w_in[c % 2], 16)

            for c in range(8):
                load_chunk(0, c, first=(c < 2))
                if c == 1:
                    sp.wait_ge(num_done, 4 * PAIRS)
                    for row, src in ((bout_row, b_out), (battn_row, attn_b), (bnext_row, next_b)):
                        sp.dma_start(row, src.partition_broadcast(P)).then_inc(rows_in, 16)
                    sp.dma_start(x_res, x_e[:, :, 0, :]).then_inc(x_res_in, 16)
            with sp.Fori(1, E) as e:
                for c in range(8):
                    load_chunk(e, c)
                    if c == 0:
                        sp.wait_ge(xl_lo_done, e)
                        sp.dma_start(x_res, x_e[:, :, e, :]).then_inc(x_res_in, 16)

        @block.gpsimd
        def _(pool):
            pool.memset(ident[:, :], 0.0).then_inc(ident_made, 1)
            pool.memset(ident_b[:, :], 0.0).then_inc(ident_made, 1)
            pool.wait_ge(ident_made, 2)
            for m in (ident, ident_b):
                pool.affine_select(out=m[:, :], in_=m[:, :], compare_op=ALU.not_equal, fill=1.0, base=0,
                                   pattern=[[-1, P]], channel_multiplier=1).then_inc(ident_made, 1)
            pool.dma_start(b1_rows, b1.rearrange("e (f p) -> (e f) p", p=P)).then_inc(cols_in, 16)
            pool.dma_start(vec_rows[0:E * K], b2.rearrange("e (k p) -> (e k) p", p=P)).then_inc(cols_in, 16)
            pool.dma_start(vec_rows[E * K:E * K + K], ln_g.rearrange("(k p) -> k p", p=P)).then_inc(cols_in, 16)
            pool.dma_start(vec_rows[E * K + K:VEC], ln_b.rearrange("(k p) -> k p", p=P)).then_inc(cols_in, 16)
            for i, w in enumerate((w_out, attn_w, next_w)):
                hi, lo = fixed[i]
                flat_hi, flat_lo = (a.rearrange("p k n -> p (k n)") for a in (hi, lo))
                if i:
                    pool.wait_ge(wother_step, 3 * i)
                pool.dma_start(wother_f.rearrange("p (k n) -> p k n", k=K),
                               w.rearrange("(k p) n -> p k n", p=P)).then_inc(wother_in, 16)
                pool.wait_ge(wother_in, 16 * (i + 1))
                pool.tensor_scalar(wother_f, wother_f, WS, 1.0, ALU.mult, ALU.mult).then_inc(wother_step, 1)
                pool.wait_ge(wother_step, 3 * i + 1)
                pool.tensor_copy(flat_hi, wother_f).then_inc(wother_step, 1)
                pool.wait_ge(wother_step, 3 * i + 2)
                pool.tensor_tensor(flat_lo, wother_f, flat_hi, ALU.subtract).then_inc(wother_step, 1)
            pool.wait_ge(sT_evac, T)
            pool.dma_start(s1T_dram, s1T[0:H, :]).then_inc(s1T_out, 16)
            pool.wait_ge(smax_done, 1)
            pool.partition_all_reduce(smax_all[:, :], smax[:, :], P, bass.bass_isa.ReduceOp.max)\
                .then_inc(smax_all_done, 1)
            with pool.Fori(0, E) as e:
                pool.wait_ge(out_ready, e + 1)
                pool.dma_start(out_e[:, :, e, :], y_rows).then_inc(out_stored, 16)
            pool.wait_ge(out_stored, 16 * E)

        @block.tensor
        def _(pe):
            def three(outp, a_hi, a_lo, b_hi, b_lo, start, stop, **kw):
                pe.matmul(outp, a_hi, b_hi, start=start, stop=False, **kw)
                pe.matmul(outp, a_hi, b_lo, start=False, stop=False, **kw)
                return pe.matmul(outp, a_lo, b_hi, start=False, stop=stop, **kw)

            pe.wait_ge(ident_made, 4)
            pe.wait_ge(cols_in, 64)
            pe.transpose(ps[:, 7, 0:P], b1_rows, ident[:, :])
            pe.transpose(ps[:, 7, P:P + VEC], vec_rows[0:VEC], ident[0:VEC, 0:VEC]).then_inc(cols_turned, 1)

            def lead(t, u, first=False):
                pe.wait_ge(xn_ready, t + 1)
                if not first:
                    pe.wait_ge(xlo_done, t - 1)
                for k in range(K):
                    last = pe.transpose(ps[:, u, k * P:(k + 1) * P], xn0[u][:, k * P:(k + 1) * P], ident[:, :])
                last.then_inc(xT_done, 1)

            def lag(t, u, first=False):
                pe.wait_ge(xlo_done, t + 1)
                if not first:
                    pe.wait_ge(s_evac, t)
                else:
                    pe.wait_ge(wseq_lo_done, 1)
                    pe.wait_ge(wa_step, 6)
                    pe.wait_ge(cols_evac, 3)
                for k in range(K):
                    last = three(ps[:, 4, 0:2 * H], xnT_hi[u][:, k], xnT_lo[u][:, k], wa_hi[:, k], wa_lo[:, k],
                                 k == 0, k == K - 1)
                last.then_inc(s_done, 1)
                for k in range(K):
                    last = three(ps[:, 2 + u, :], xnT_hi[u][:, k], xnT_lo[u][:, k], wseq_hi[:, k], wseq_lo[:, k],
                                 k == 0, k == K - 1)
                last.then_inc(seq_done, 1)
                pe.wait_ge(adj_bin, t + 1)
                for half, (read, done) in enumerate(((mask_dve, adjT_a), (mask_act, adjT_b))):
                    if not first:
                        pe.wait_ge(read, t)
                    for j in range(8):
                        jj = 8 * half + j
                        last = pe.transpose(ps_adjT[half][:, j, :], adj_b[u][:, jj * P:(jj + 1) * P], ident_b[:, :])
                    last.then_inc(done, 1)
                pe.wait_ge(s_evac, t + 1)
                if not first:
                    pe.wait_ge(sT_evac, t)
                pe.transpose(ps[0:H, 5, 0:P], s1_now[u][:, :], ident[:, :]).then_inc(sT_done, 1)

            lead(0, 0, first=True)
            lead(1, 1, first=True)
            lag(0, 0, first=True)
            with pe.Fori(0, T // 2 - 1) as i:
                lead(2 * i + 2, 0)
                lag(2 * i + 1, 1)
                lead(2 * i + 3, 1)
                lag(2 * i + 2, 0)
            lag(T - 1, 1)

            def pair(q, wb, first=False):
                w = w_att[wb]
                pe.wait_ge(w_ready, 2 * q + 2)
                for b in range(2):
                    for g in range(2):
                        group = 4 * q + 2 * b + g
                        if not (first and b == 0):
                            pe.wait_ge(acc_free, group - 1)
                        else:
                            pe.wait_ge(mask_act, T)
                            pe.wait_ge(mask_dve, T)
                            pe.wait_ge(coef_step, 9)
                        for c in range(T // 2):
                            if g == 0:
                                pe.wait_ge(g_ready, 16 * q + 8 * b + c + 1)
                            if g == 0 or c == 0:
                                settle(pe)
                            for j in (2 * c, 2 * c + 1):
                                for a in range(4):
                                    acc = ps[:, 4 * g + a, 0:8 * V1]
                                    cols = slice((4 * g + a) * P, (4 * g + a + 1) * P)
                                    for hh in range(2):
                                        last_g = pe.matmul(acc[:, hh * 4 * V1:(hh + 1) * 4 * V1],
                                                           g_f8[b][:, j, hh, cols], w[:, j, hh, :],
                                                           start=(j == 0 and hh == 0), stop=False,
                                                           skip_group_check=True)
                                    rows = slice(b * HALF + (4 * g + a) * P, b * HALF + (4 * g + a + 1) * P)
                                    last_m = pe.matmul(acc.rearrange("p (x k c) -> p x k c", k=2, c=V1)[:, :, 1, :],
                                                       mask_f8[:, j, rows],
                                                       w[:, j].rearrange("p h (x k c) -> p (h x) k c", k=2, c=V1)[:, :, 1, :],
                                                       start=False, stop=(j == T - 1), skip_group_check=True)
                            if g == 1:
                                last_g.then_inc(g_free, 1)
                        last_m.then_inc(acc_done, 1)

            pair(0, 0, first=True)
            pair(1, 1)
            with pe.Fori(0, PAIRS // 2 - 1) as i:
                pair(2 * i + 2, 0)
                pair(2 * i + 3, 1)

            def transpose_rows(src, n, ready, count, first=False):
                pe.wait_ge(ready, count)
                if not first:
                    pe.wait_ge(tr_free, n)
                for k in range(K):
                    for u in range(2):
                        last = pe.transpose(ps_tr[:, k, u * P:(u + 1) * P], src[:, u, k * P:(k + 1) * P], ident[:, :])
                last.then_inc(tr_done, 1)

            def project(a_hi, a_lo, b_hi, b_lo, done):
                for u in range(2):
                    for k in range(K):
                        rows = slice(u * P, (u + 1) * P)
                        last = three(ps_mm[:, u, :], a_hi[:, k, rows], a_lo[:, k, rows], b_hi[:, k], b_lo[:, k],
                                     k == 0, k == K - 1)
                last.then_inc(done, 1)

            def w1_tiles(e, fp, first=False):
                c = fp // 2
                if fp % 2 == 0:
                    pe.wait_ge(wlo_done, 8 * e + c + 1)
                if fp == 0:
                    pe.wait_ge(tr_free, 3 * e + 3)
                if not (first and fp < 2):
                    pe.wait_ge(h_gelu, 8 * e + fp - 1)
                for f in range(2):
                    cols = slice((2 * fp + f) % 4 * P, ((2 * fp + f) % 4 + 1) * P)
                    for k in range(K):
                        last = three(ps_h[fp % 2][:, f, :], wpart_hi[c][:, k, cols], wpart_lo[c][:, k, cols],
                                     xaT_hi[:, k], xaT_lo[:, k], k == 0, k == K - 1)
                last.then_inc(h_done, 1)

            def w2_chunk(e, c, first):
                pe.wait_ge(wlo_done, 8 * e + c + 5)
                pe.wait_ge(hlo_done, 8 * e + 2 * c + 2)
                if c == 0 and not first:
                    pe.wait_ge(y_free, e)
                order = [(f, d) for dp in range(2) for f in range(4) for d in (2 * dp, 2 * dp + 1)] if c == 3 \
                    else [(f, d) for f in range(4) for d in range(4)]
                for f, d in order:
                    ft = 4 * c + f
                    last = three(ps_y[:, d, :], wpart_hi[4 + c][:, f, d * P:(d + 1) * P],
                                 wpart_lo[4 + c][:, f, d * P:(d + 1) * P], h_hi[:, ft], h_lo[:, ft],
                                 ft == 0 and d % 2 == 0, ft == FT - 1, skip_group_check=True)
                last.then_inc(y_done, 1)

            def step(e, ffn=True, ahead=True, first=False):
                n = e + 1
                if ahead:
                    transpose_rows(hid, 3 * n, hid_ready, n + 1, first=not ffn)
                if ffn:
                    w1_tiles(e, 0, first)
                    w1_tiles(e, 1, first)
                if ahead:
                    pe.wait_ge(tr_free, 3 * n + 1)
                    if ffn and not first:
                        pe.wait_ge(nx_free, e)
                    project(hidT_hi, hidT_lo, wout_hi, wout_lo, mo_done)
                if ffn:
                    for fp in range(2, 6):
                        w1_tiles(e, fp)
                if ahead:
                    transpose_rows(z, 3 * n + 1, xh_ready, n + 1)
                if ffn:
                    w1_tiles(e, 6)
                    w1_tiles(e, 7)
                    for c in range(4):
                        w2_chunk(e, c, first)
                if ahead:
                    pe.wait_ge(xl_lo_done, n + 1)
                    pe.wait_ge(mo_free, n + 1)
                    project(xlT_hi, xlT_lo, wattn_hi, wattn_lo, ma_done)
                if ffn:
                    pe.wait_ge(ylo_done, e + 1)
                    if ahead:
                        pe.wait_ge(ma_free, n + 1)
                    else:
                        pe.wait_ge(nx_free, e)
                    project(yT_hi, yT_lo, wnext_hi, wnext_lo, nx_done)
                if ahead:
                    transpose_rows(z, 3 * n + 2, xa_ready, n + 1)

            pe.wait_ge(acc_free, 4 * PAIRS)
            pe.wait_ge(wother_step, 9)
            step(-1, ffn=False)
            step(0, first=True)
            with pe.Fori(1, E - 1) as e:
                step(e)
            step(E - 1, ahead=False)

        @block.scalar
        def _(act):
            act.wait_ge(wseq_in, 16)
            act.activation(wseq_hi, wseq_f, ACT.Copy, scale=WS).then_inc(wseq_hi_done, 1)
            act.wait_ge(ln_step, 3)
            act.activation(ln_s[:, :], ln_v[:, :], ACT.Sqrt).then_inc(sqrt_done, 1)

            def cast(t, u, count, first=False):
                act.wait_ge(adj_in[u], 16 * count)
                if not first:
                    act.wait_ge(adjT_b, t - 1)
                act.activation(adj_b[u], adj_f[u], ACT.Copy, accum_out=rowsum[:, u:u + 1]).then_inc(adj_cast, 1)

            def lead(t, u, first=False):
                act.wait_ge(xT_done, t + 1)
                if not first:
                    act.wait_ge(seq_done, t - 1)
                act.activation(xnT_hi[u].rearrange("p k c -> p (k c)"), ps[:, u, :], ACT.Copy, scale=XS)\
                    .then_inc(xhi_done, 1)

            def lag(t):
                act.wait_ge(adjT_b, t + 1)
                act.activation(mask_u8[:, 8:16, bass.ds(t * P, P)], ps_adjT[1], ACT.Copy, scale=NEG1)\
                    .then_inc(mask_act, 1)
                act.wait_ge(sT_done, t + 1)
                act.activation(s1T[0:H, bass.ds(t * P, P)], ps[0:H, 5, 0:P], ACT.Copy).then_inc(sT_evac, 1)

            cast(0, 0, 1, first=True)
            cast(1, 1, 1, first=True)
            lead(0, 0, first=True)
            lead(1, 1, first=True)
            lag(0)
            with act.Fori(0, T // 2 - 1) as i:
                cast(2 * i + 2, 0, i + 2)
                lead(2 * i + 2, 0)
                lag(2 * i + 1)
                cast(2 * i + 3, 1, i + 2)
                lead(2 * i + 3, 1)
                lag(2 * i + 2)
            lag(T - 1)

            act.wait_ge(coef_step, 3)
            act.activation(e_b, su, ACT.Exp).then_inc(exp_done, 1)
            act.activation(e_d, su, ACT.Exp, scale=0.2).then_inc(exp_done, 1)
            act.wait_ge(coef_step, 6)
            act.activation(a_c[:, :, :, 0], st_a, ACT.Exp).then_inc(exp_done, 1)
            act.activation(a_c[:, :, :, 1], st_c, ACT.Exp).then_inc(exp_done, 1)

            def copy_low(q, b, g):
                group = 4 * q + 2 * b + g
                act.wait_ge(acc_done, group + 1)
                act.activation(acc_lo[g], ps[:, 4 * g:4 * g + 4, 0:8 * V1]
                               .rearrange("p a (h x c) -> p a h x c", h=2, x=2)[:, :, :, 1, :], ACT.Copy)\
                    .then_inc(lo_copied, 1)

            def compare_unit(q, b, tb, evac, free):
                act.wait_ge(s1_row_in[b], 16 * (q + 1))
                for c in range(T // 2):
                    if evac and c in (0, 4):
                        copy_low(q - 1, b, c // 4)
                    if free:
                        act.wait_ge(g_free, 16 * (q - 1) + 8 * b + c + 1)
                    if free or c == 0:
                        settle(act)
                    for j in (2 * c, 2 * c + 1):
                        for hh in range(2):
                            if (j % 4, hh) not in DVE_CMP:
                                last = act.activation(g_f8[b][:, j, hh, :], s1_row[b][:, hh, :], ACT.Sigmoid,
                                                      bias=thr_now[tb][:, 1, j, hh:hh + 1], scale=BIG,
                                                      saturate=False)
                    last.then_inc(act_cmp, 1)

            def pair(q, tb, evac=True):
                act.wait_ge(thr_ready, q + 1)
                for b in range(2):
                    compare_unit(q, b, tb, evac, evac)

            act.wait_ge(adjT_b, T)
            pair(0, 0, evac=False)
            pair(1, 1)
            with act.Fori(0, PAIRS // 2 - 1) as i:
                pair(2 * i + 2, 0)
                pair(2 * i + 3, 1)
            for b in range(2):
                for g in range(2):
                    copy_low(PAIRS - 1, b, g)

            def split_chunk(e, c, first=False):
                act.wait_ge(w_in[c % 2], 16 * (4 * e + c // 2 + 1))
                if not first:
                    if c < 4:
                        act.wait_ge(h_done, 8 * (e - 1) + 2 * c + 2)
                    else:
                        act.wait_ge(y_done, 4 * (e - 1) + c - 3)
                act.activation(wpart_hi[c], w_stage[c % 2], ACT.Copy, scale=WS).then_inc(whi_done, 1)

            def transposed_hi(dst, n):
                act.wait_ge(tr_done, n + 1)
                act.activation(dst, ps_tr, ACT.Copy, scale=XS).then_inc(tr_hi, 1)

            def gelu(e, fp, first=False):
                act.wait_ge(h_done, 8 * e + fp + 1)
                if not (first and fp < 2):
                    act.wait_ge(hlo_done, 8 * e + fp - 1)
                for f in range(2):
                    bias = b1_col[:, bass.ds(e, 1), 2 * fp + f:2 * fp + f + 1].rearrange("p a b -> p (a b)")
                    last = act.activation(h_f[fp % 2][:, f, :], ps_h[fp % 2][:, f, :], ACT.Gelu,
                                          bias=bias, scale=1.0 / (WS * XS))
                last.then_inc(h_gelu, 1)

            def norm_root(n):
                act.wait_ge(norm_step, n)
                act.activation(ln_s[:, 0:2], ln_v[:, 0:2], ACT.Sqrt).then_inc(norm_sqrt, 1)

            def step(e, ffn=True, ahead=True, first=False):
                n = e + 1
                if ahead:
                    transposed_hi(hidT_hi, 3 * n)
                if ffn:
                    gelu(e, 0, first)
                    gelu(e, 1, first)
                if ahead:
                    split_chunk(n, 0, not ffn)
                    act.wait_ge(neg_ready, n + 1)
                    act.activation(en, en, ACT.Exp).then_inc(en_ready, 1)
                if ffn:
                    gelu(e, 2)
                if ahead:
                    norm_root(15 * n + 3)
                if ffn:
                    gelu(e, 3)
                if ahead:
                    split_chunk(n, 1, not ffn)
                    norm_root(15 * n + 11)
                if ffn:
                    gelu(e, 4)
                    gelu(e, 5)
                if ahead:
                    split_chunk(n, 2, not ffn)
                    act.wait_ge(tr_free, 3 * n + 2)
                    act.activation(xlT_hi, xl, ACT.Copy, scale=XS).then_inc(xl_hi_done, 1)
                if ffn:
                    gelu(e, 6)
                    gelu(e, 7)
                if ahead:
                    for c in range(3, 7):
                        split_chunk(n, c, not ffn)
                if ffn:
                    act.wait_ge(nx_free, e + 1)
                    act.activation(y_rows, y_rows, ACT.Gelu).then_inc(og_ready, 1)
                if ahead:
                    transposed_hi(xaT_hi, 3 * n + 2)
                    split_chunk(n, 7, not ffn)

            act.wait_ge(cols_evac, 3)
            act.wait_ge(acc_done, 4 * PAIRS)
            step(-1, ffn=False)
            step(0, first=True)
            with act.Fori(1, E - 1) as e:
                step(e)
            step(E - 1, ahead=False)

        @block.vector
        def _(dve):
            def inverse_std(v, s, t, r, step, at, root, root_at):
                dve.wait_ge(root, root_at)
                dve.reciprocal(t, s).then_inc(step, 1)
                dve.wait_ge(step, at + 1)
                dve.tensor_tensor(t, t, v, ALU.mult).then_inc(step, 1)
                dve.wait_ge(step, at + 2)
                dve.tensor_tensor(t, t, s, ALU.add).then_inc(step, 1)
                dve.wait_ge(step, at + 3)
                dve.reciprocal(r, t).then_inc(step, 1)
                dve.wait_ge(step, at + 4)

            for t in range(T):
                if t % 4 == 0:
                    dve.wait_ge(x_in[t // 4], 16)
                last = dve.bn_stats(stats[:, t, :], x_all[:, t, :])
            last.then_inc(ln_step, 1)
            dve.wait_ge(ln_step, 1)
            for t in range(T):
                last = dve.bn_aggr(mv[:, t, :], stats[:, t, :])
            last.then_inc(ln_step, 1)
            dve.wait_ge(ln_step, 2)
            dve.tensor_scalar(ln_v[:, :], mv[:, :, 1], 0.25, 0.25 * EPS, ALU.mult, ALU.add).then_inc(ln_step, 1)
            dve.wait_ge(wseq_hi_done, 1)
            dve.scalar_tensor_tensor(wseq_lo, wseq_f, WS, wseq_hi, ALU.mult, ALU.subtract).then_inc(wseq_lo_done, 1)
            dve.wait_ge(a_in, 32)
            for i in range(2):
                dve.tensor_tensor(wa_prod, wseq_f.rearrange("p k (h c) -> p (k h) c", c=DH),
                                  a_row[:, i:i + 1, :].to_broadcast([P, K * H, DH]), ALU.mult).then_inc(wa_step, 1)
                dve.wait_ge(wa_step, 2 * i + 1)
                dve.tensor_reduce(wa_f[:, :, i, :], wa_prod.rearrange("p (k h) c -> p k h c", h=H), AX.X, ALU.add)\
                    .then_inc(wa_step, 1)
                dve.wait_ge(wa_step, 2 * i + 2)
            wa_flat, wah_flat, wal_flat = (wa_f.rearrange("p k i h -> p (k i h)"),
                                           wa_hi.rearrange("p k c -> p (k c)"), wa_lo.rearrange("p k c -> p (k c)"))
            dve.tensor_scalar(wah_flat, wa_flat, WS, None, ALU.mult).then_inc(wa_step, 1)
            dve.wait_ge(wa_step, 5)
            dve.scalar_tensor_tensor(wal_flat, wa_flat, WS, wah_flat, ALU.mult, ALU.subtract).then_inc(wa_step, 1)
            dve.memset(seqv[:, :, DH::V1], 1.0)
            dve.wait_ge(cols_turned, 1)
            dve.tensor_copy(b1_col[:, :, :].rearrange("p e f -> p (e f)"), ps[:, 7, 0:P]).then_inc(cols_evac, 1)
            dve.tensor_scalar(vec_col[:, 0:E * K], ps[:, 7, P:P + E * K], HS, None, ALU.mult).then_inc(cols_evac, 1)
            dve.tensor_copy(vec_col[:, E * K:VEC], ps[:, 7, P + E * K:P + VEC]).then_inc(cols_evac, 1)
            dve.wait_ge(ln_step, 3)
            inverse_std(ln_v[:, :], ln_s[:, :], ln_t[:, :], ln_r[:, :], ln_step, 3, sqrt_done, 1)

            def lead_xn(t, u, first=False):
                if not first:
                    dve.wait_ge(xT_done, t - 1)
                mean = mv[:, bass.ds(t, 1), 0:1].rearrange("p a b -> p (a b)")
                dve.tensor_scalar(xn0[u], x_all[:, bass.ds(t, 1), :].rearrange("p t d -> p (t d)"), mean,
                                  ln_r[:, bass.ds(t, 1)], ALU.subtract, ALU.mult).then_inc(xn_ready, 1)

            def lead_adj(t, u):
                dve.wait_ge(adj_cast, t + 1)
                dve.tensor_scalar(lonely[:, u:u + 1], rowsum[:, u:u + 1], 0.5, None, ALU.is_lt).then_inc(lonely_done, 1)
                dve.wait_ge(lonely_done, t + 1)
                dve.tensor_scalar(adj_b[u], adj_b[u], lonely[:, u:u + 1], None, ALU.max).then_inc(adj_bin, 1)

            def lead_lo(t, u):
                dve.wait_ge(xhi_done, t + 1)
                dve.scalar_tensor_tensor(xnT_lo[u].rearrange("p k c -> p (k c)"), ps[:, u, :], XS,
                                         xnT_hi[u].rearrange("p k c -> p (k c)"), ALU.mult, ALU.subtract)\
                    .then_inc(xlo_done, 1)

            def lag_mask(t):
                dve.wait_ge(adjT_a, t + 1)
                dve.tensor_scalar(mask_u8[:, 0:8, bass.ds(t * P, P)], ps_adjT[0], NEG1, None, ALU.mult)\
                    .then_inc(mask_dve, 1)

            def lag_seq(t, u):
                dve.wait_ge(s_done, t + 1)
                dve.tensor_scalar(s1_now[u][:, :], ps[:, 4, 0:H], 1.0 / (WS * XS), None, ALU.mult)
                dve.tensor_scalar(s12[:, bass.ds(t, 1), :].rearrange("p t h -> p (t h)"), ps[:, 4, 0:2 * H],
                                  1.0 / (WS * XS), None, ALU.mult).then_inc(s_evac, 1)
                dve.wait_ge(seq_done, t + 1)
                dve.tensor_scalar(seqv[:, bass.ds(t, 1), :].rearrange("p t (h c) -> p (t h) c", c=V1)[:, :, 0:DH],
                                  ps[:, 2 + u, :].rearrange("p (h c) -> p h c", c=DH),
                                  1.0 / (WS * XS), None, ALU.mult).then_inc(seq_evac, 1)

            lead_xn(0, 0, first=True)
            lead_xn(1, 1, first=True)
            lead_adj(0, 0)
            lead_adj(1, 1)
            lead_lo(0, 0)
            lead_lo(1, 1)
            lag_mask(0)
            lag_seq(0, 0)
            with dve.Fori(0, T // 2 - 1) as i:
                for t, u in ((2 * i + 2, 0), (2 * i + 3, 1)):
                    lead_xn(t, u)
                    lead_adj(t, u)
                    lag_mask(t - 1)
                    lead_lo(t, u)
                    lag_seq(t - 1, 1 - u)
            lag_mask(T - 1)
            lag_seq(T - 1, 1)

            dve.wait_ge(s_evac, T)
            s1, s2 = s12[:, :, 0:H], s12[:, :, H:2 * H]
            dve.tensor_reduce(smax[:, :], s2.rearrange("p t h -> p h t"), AX.X, ALU.max).then_inc(smax_done, 1)
            by_pair = s2.rearrange("p t (q h) -> p t q h", h=2)
            for kind, factor in ((0, -1.0), (1, BIG)):
                dve.tensor_scalar(thr[:, :, kind].rearrange("p q t h -> p t q h"), by_pair, factor, None, ALU.mult)\
                    .then_inc(coef_step, 1)
            dve.wait_ge(smax_all_done, 1)
            top = smax_all[:, :].unsqueeze(1).to_broadcast([P, T, H])
            dve.tensor_tensor(su, s2, top, ALU.subtract).then_inc(coef_step, 1)
            dve.tensor_tensor(st_a, s1, top, ALU.add).then_inc(coef_step, 1)
            dve.wait_ge(coef_step, 4)
            dve.tensor_scalar(st_c, st_a, -0.8, 0.0, ALU.mult, ALU.min).then_inc(coef_step, 1)
            dve.wait_ge(coef_step, 5)
            dve.tensor_scalar(st_a, st_a, 0.8, 0.0, ALU.mult, ALU.min).then_inc(coef_step, 1)
            dve.wait_ge(exp_done, 2)
            dve.tensor_scalar(e_b, e_b, KAPPA, None, ALU.mult).then_inc(coef_step, 1)
            dve.tensor_scalar(e_d, e_d, -KAPPA, None, ALU.mult).then_inc(coef_step, 1)
            dve.wait_ge(seq_evac, T)
            dve.wait_ge(coef_step, 8)
            dve.wait_ge(exp_done, 4)
            dve.tensor_copy(rden[:, :, :], s12[:, 0:2, 0:H]).then_inc(coef_step, 1)

            def make_w(q, wb, first=False):
                dve.tensor_copy(thr_now[wb][:, :, :, :].rearrange("p k t h -> p (k t h)"),
                                thr[:, bass.ds(q, 1)].rearrange("p q k t h -> p (q k t h)")).then_inc(thr_ready, 1)
                for jb in range(2):
                    js = slice(8 * jb, 8 * jb + 8)
                    if not first or jb:
                        dve.wait_ge(w_ready, 2 * q + jb)
                    v = seqv[:, js, bass.ds(2 * q * V1, 2 * V1)].rearrange("p t (h c) -> p t h c", c=V1)
                    for kind, coef in ((0, e_b), (1, e_d)):
                        f = coef[:, js, bass.ds(2 * q, 2)].unsqueeze(3).to_broadcast([P, 8, 2, V1])
                        dve.tensor_tensor(w_prod[:, :, :, kind * V1:(kind + 1) * V1], v, f, ALU.mult)\
                            .then_inc(w_prod_step, 1)
                    dve.wait_ge(w_prod_step, 6 * q + 3 * jb + 2)
                    hi, lo = w_att[wb][:, js, :, 0:2 * V1], w_att[wb][:, js, :, 2 * V1:4 * V1]
                    dve.tensor_copy(hi, w_prod).then_inc(w_prod_step, 1)
                    dve.wait_ge(w_prod_step, 6 * q + 3 * jb + 3)
                    dve.tensor_tensor(lo, w_prod, hi, ALU.subtract).then_inc(w_ready, 1)

            def acc_add(q, b, g):
                group = 4 * q + 2 * b + g
                dve.wait_ge(lo_copied, group + 1)
                dve.tensor_tensor(acc_s[g], ps[:, 4 * g:4 * g + 4, 0:8 * V1]
                                  .rearrange("p a (h x c) -> p a h x c", h=2, x=2)[:, :, :, 0, :],
                                  acc_lo[g], ALU.add).then_inc(acc_free, 1)

            def acc_scale(q, b, g):
                group = 4 * q + 2 * b + g
                dve.wait_ge(acc_free, group + 1)
                s = acc_s[g].rearrange("p a h (k c) -> p a (h k) c", c=V1)
                t0 = 8 * b + 4 * g
                coef = a_c[:, t0:t0 + 4].rearrange("p t h k -> p t (h k)")[:, :, bass.ds(4 * q, 4)]
                dve.tensor_tensor(s, s, coef.unsqueeze(3).to_broadcast([P, 4, 4, V1]), ALU.mult)\
                    .then_inc(acc_scaled, 1)

            def acc_sum(q, b, g):
                group = 4 * q + 2 * b + g
                dve.wait_ge(acc_scaled, group + 1)
                t0 = 8 * b + 4 * g
                dst = seqv[:, t0:t0 + 4, bass.ds(2 * q * V1, 2 * V1)].rearrange("p t (h c) -> p t h c", c=V1)
                dve.tensor_tensor(dst, acc_s[g][:, :, :, 0:V1], acc_s[g][:, :, :, V1:2 * V1], ALU.add)\
                    .then_inc(num_done, 1)

            def mask_chunk(q, b, c):
                dve.wait_ge(act_cmp, 16 * q + 8 * b + c + 1)
                dve.wait_ge(dve_cmp, 16 * q + 8 * b + c + 1)
                g = g_u32[b][:, 2 * c:2 * c + 2]
                m = mask_u32[:, 2 * c:2 * c + 2, b * HALF // 4:(b + 1) * HALF // 4]
                dve.tensor_tensor(g, g, m.unsqueeze(2).to_broadcast([P, 2, 2, HALF // 4]), ALU.bitwise_and)\
                    .then_inc(g_ready, 1)

            def unit(q, b, tb, evac):
                dve.wait_ge(s1_row_in[b], 16 * (q + 1))
                for c in range(T // 2):
                    if evac and c % 4 < 3:
                        (acc_add, acc_scale, acc_sum)[c % 4](q - 1, b, c // 4)
                    if evac:
                        dve.wait_ge(g_free, 16 * (q - 1) + 8 * b + c + 1)
                    for j in (2 * c, 2 * c + 1):
                        for hh in range(2):
                            if (j % 4, hh) in DVE_CMP:
                                last = dve.tensor_scalar(g_u8[b][:, j, hh, :], s1_row[b][:, hh, :],
                                                         thr_now[tb][:, 0, j, hh:hh + 1], POS1, ALU.is_gt, ALU.mult)
                    last.then_inc(dve_cmp, 1)
                    if c:
                        mask_chunk(q, b, c - 1)
                mask_chunk(q, b, T // 2 - 1)

            def pair(q, wb, evac=True):
                make_w(q, wb, first=not evac)
                for b in range(2):
                    unit(q, b, wb, evac)

            dve.wait_ge(mask_act, T)
            dve.wait_ge(mask_dve, T)
            pair(0, 0, evac=False)
            pair(1, 1)
            with dve.Fori(0, PAIRS // 2 - 1) as i:
                pair(2 * i + 2, 0)
                pair(2 * i + 3, 1)
            for b in range(2):
                for g in range(2):
                    acc_add(PAIRS - 1, b, g)
                    acc_scale(PAIRS - 1, b, g)
                    acc_sum(PAIRS - 1, b, g)

            rows = seqv.rearrange("p (u t) c -> p u t c", u=2)

            def tiles(e, n=H * V1):
                return rows[:, :, bass.ds(e, 1), 0:n].rearrange("p u t c -> p u (t c)")

            def split_chunk(n, c):
                dve.wait_ge(whi_done, 8 * n + c + 1)
                dve.scalar_tensor_tensor(wpart_lo[c], w_stage[c % 2], WS, wpart_hi[c], ALU.mult, ALU.subtract)\
                    .then_inc(wlo_done, 1)

            def transposed_lo(dst, hi, n):
                flat = "p k c -> p (k c)"
                dve.wait_ge(tr_hi, n)
                dve.scalar_tensor_tensor(dst.rearrange(flat), ps_tr.rearrange(flat), XS, hi.rearrange(flat),
                                         ALU.mult, ALU.subtract).then_inc(tr_free, 1)

            def hidden(e):
                num = tiles(e).rearrange("p u (h c) -> p u h c", c=V1)
                dve.reciprocal(rden[:, :, :], num[:, :, :, DH]).then_inc(rden_done, 1)
                dve.wait_ge(rden_done, e + 1)
                dve.tensor_tensor(hid.rearrange("p u (h c) -> p u h c", c=DH), num[:, :, :, 0:DH],
                                  rden[:, :, :].unsqueeze(3).to_broadcast([P, 2, H, DH]), ALU.mult)\
                    .then_inc(hid_ready, 1)

            def elu_in(e):
                dve.wait_ge(mo_done, e + 1)
                dve.scalar_tensor_tensor(z, ps_mm, 1.0 / (WS * XS), bout_row.unsqueeze(1).to_broadcast([P, 2, D]),
                                         ALU.mult, ALU.add).then_inc(mo_free, 1)
                dve.wait_ge(mo_free, e + 1)
                dve.tensor_scalar(en, z, 0.0, None, ALU.min).then_inc(neg_ready, 1)

            def statistics(src, at):
                settle(dve)
                for u in range(2):
                    last = dve.bn_stats(stats[:, u, :], src[:, u, :])
                last.then_inc(norm_step, 1)
                dve.wait_ge(norm_step, at + 1)
                settle(dve)
                for u in range(2):
                    last = dve.bn_aggr(mv[:, u, :], stats[:, u, :])
                last.then_inc(norm_step, 1)
                dve.wait_ge(norm_step, at + 2)
                dve.tensor_scalar(ln_v[:, 0:2], mv[:, 0:2, 1], 0.25, 0.25 * EPS, ALU.mult, ALU.add)\
                    .then_inc(norm_step, 1)
                dve.wait_ge(norm_step, at + 3)

            def normalise(dst, src, at, root_at):
                inverse_std(ln_v[:, 0:2], ln_s[:, 0:2], ln_t[:, 0:2], ln_r[:, 0:2], norm_step, at + 3,
                            norm_sqrt, root_at)
                for u in range(2):
                    last = dve.tensor_scalar(dst[:, u, :], src[:, u, :], mv[:, u, 0:1], ln_r[:, u:u + 1],
                                             ALU.subtract, ALU.mult)
                return last

            def elu_out(e):
                dve.wait_ge(en_ready, e + 1)
                dve.scalar_tensor_tensor(z, z, 0.0, en, ALU.max, ALU.add).then_inc(elu_step, 1)
                dve.wait_ge(elu_step, 2 * e + 1)
                dve.wait_ge(x_res_in, 16 * (e + 1))
                x1 = tiles(e, D)
                dve.scalar_tensor_tensor(x1, z, -1.0, x_res, ALU.add, ALU.add).then_inc(elu_step, 1)
                dve.wait_ge(elu_step, 2 * e + 2)
                statistics(x1, 15 * e)

            def norm_1(e):
                normalise(xn, tiles(e, D), 15 * e, 2 * e + 1).then_inc(norm_step, 1)
                dve.wait_ge(norm_step, 15 * e + 8)
                statistics(xn, 15 * e + 8)

            def norm_2(e):
                normalise(z, xn, 15 * e + 8, 2 * e + 2).then_inc(xh_ready, 1)

            def gain(e):
                dve.wait_ge(tr_done, 3 * e + 2)
                for k in range(K):
                    last = dve.tensor_scalar(xl[:, k, :], ps_tr[:, k, :], g_col[:, k:k + 1], b_col[:, k:k + 1],
                                             ALU.mult, ALU.add)
                last.then_inc(tr_free, 1)

            def gain_lo(e):
                dve.wait_ge(xl_hi_done, e + 1)
                dve.scalar_tensor_tensor(xlT_lo, xl, XS, xlT_hi, ALU.mult, ALU.subtract).then_inc(xl_lo_done, 1)

            def dense_out(e):
                dve.wait_ge(ma_done, e + 1)
                dve.scalar_tensor_tensor(z, ps_mm, 1.0 / (WS * XS), battn_row.unsqueeze(1).to_broadcast([P, 2, D]),
                                         ALU.mult, ALU.add).then_inc(ma_free, 1)
                dve.wait_ge(ma_free, e + 1)
                dve.tensor_tensor(z, z, xn, ALU.add).then_inc(xa_ready, 1)

            def split_h(e, fp, first):
                dve.wait_ge(h_gelu, 8 * e + fp + 1)
                if not first:
                    dve.wait_ge(y_done, 4 * e)
                pair_of = slice(2 * fp, 2 * fp + 2)
                dve.tensor_scalar(h_hi[:, pair_of], h_f[fp % 2], HS, None, ALU.mult).then_inc(hhi_done, 1)
                dve.wait_ge(hhi_done, 8 * e + fp + 1)
                dve.scalar_tensor_tensor(h_lo[:, pair_of], h_f[fp % 2], HS, h_hi[:, pair_of],
                                         ALU.mult, ALU.subtract).then_inc(hlo_done, 1)

            def y_out(e, first):
                dve.wait_ge(y_done, 4 * e + 4)
                if not first:
                    dve.wait_ge(out_stored, 16 * e)
                for k in range(K):
                    bias = b2_col[:, bass.ds(e, 1), k:k + 1].rearrange("p a b -> p (a b)")
                    last = dve.tensor_scalar(y_f[:, k, :], ps_y[:, k, :], 1.0 / WS, bias, ALU.mult, ALU.add)
                last.then_inc(y_free, 1)
                dve.wait_ge(y_free, e + 1)
                dve.tensor_copy(yT_hi, y_f).then_inc(yhi_done, 1)
                dve.wait_ge(yhi_done, e + 1)
                dve.tensor_tensor(yT_lo, y_f, yT_hi, ALU.subtract).then_inc(ylo_done, 1)

            def next_out(e):
                dve.wait_ge(nx_done, e + 1)
                dve.scalar_tensor_tensor(y_rows, ps_mm, 1.0 / (WS * HS), bnext_row.unsqueeze(1).to_broadcast([P, 2, D]),
                                         ALU.mult, ALU.add).then_inc(nx_free, 1)

            def residual_out(e):
                dve.wait_ge(og_ready, e + 1)
                dve.tensor_tensor(y_rows, y_rows, tiles(e, D), ALU.add).then_inc(out_ready, 1)

            def step(e, ffn=True, ahead=True, first=False):
                n = e + 1
                if ahead:
                    hidden(n)
                    transposed_lo(hidT_lo, hidT_hi, 2 * n + 1)
                if ffn:
                    split_h(e, 0, first)
                    split_h(e, 1, first)
                if ahead:
                    split_chunk(n, 0)
                    elu_in(n)
                if ffn:
                    split_h(e, 2, first)
                if ahead:
                    elu_out(n)
                if ffn:
                    split_h(e, 3, first)
                if ahead:
                    split_chunk(n, 1)
                    norm_1(n)
                if ffn:
                    split_h(e, 4, first)
                if ahead:
                    norm_2(n)
                if ffn:
                    split_h(e, 5, first)
                if ahead:
                    split_chunk(n, 2)
                    gain(n)
                if ffn:
                    split_h(e, 6, first)
                if ahead:
                    gain_lo(n)
                if ffn:
                    split_h(e, 7, first)
                if ahead:
                    for c in range(3, 7):
                        split_chunk(n, c)
                if ffn:
                    y_out(e, first)
                if ahead:
                    dense_out(n)
                if ffn:
                    next_out(e)
                if ahead:
                    transposed_lo(xaT_lo, xaT_hi, 2 * n + 2)
                if ffn:
                    residual_out(e)
                if ahead:
                    split_chunk(n, 7)

            dve.wait_ge(num_done, 4 * PAIRS)
            dve.wait_ge(rows_in, 48)
            step(-1, ffn=False)
            step(0, first=True)
            with dve.Fori(1, E - 1) as e:
                step(e)
            step(E - 1, ahead=False)


_USED = ["x", "adj", "L0_gnn_W_seq", "L0_gnn_a1", "L0_gnn_a2", "L0_gnn_W_out", "L0_gnn_b_out",
         "L0_ffn_ln_g", "L0_ffn_ln_b", "L0_ffn_attn_w", "L0_ffn_attn_b", "L0_ffn_w1", "L0_ffn_b1",
         "L0_ffn_w2", "L0_ffn_b2", "L0_ffn_next_w", "L0_ffn_next_b"]


def kernel(**inputs):
    import numpy as _np
    import concourse.bacc as _bacc
    from concourse.bass_utils import run_bass_kernel_spmd as _run

    nc = _bacc.Bacc("TRN2", target_bir_lowering=False, num_devices=1)
    arrays, args = {}, []
    for name in _USED:
        a = _np.ascontiguousarray(inputs[name])
        arrays[f"in_{name}"] = a
        args.append(nc.dram_tensor(f"in_{name}", a.shape, mybir.dt.from_np(a.dtype), kind="ExternalInput").ap())
    out = nc.dram_tensor("out_rows", (N, D), F32, kind="ExternalOutput").ap()
    gat_moe_kernel(nc, *args, out)
    r = _run(nc, [arrays], core_ids=[0])
    return r.results[0]["out_rows"]
```

```python
from contextlib import ExitStack

import concourse.bass as bass
from concourse import mybir

F32 = mybir.dt.float32
F16 = mybir.dt.float16
BF16 = mybir.dt.bfloat16
F8 = mybir.dt.float8e4
U8 = mybir.dt.uint8
U32 = mybir.dt.uint32
ALU = mybir.AluOpType
ACT = mybir.ActivationFunctionType
AX = mybir.AxisListType

P = 128
N = 2048
D = 512
H = 16
DH = D // H
V1 = DH + 1
T = N // P
K = D // P
E = 8
F = 2048
FT = F // P
HALF = N // 2
PAIRS = H // 2
VEC = E * K + 2 * K
EPS = 1e-5

WS = 2.0 ** 10
XS = 2.0 ** 8
HS = 2.0 ** 6
KAPPA = 2.0 ** 10
BIG = 2.0 ** 100
NEG1 = 184.0
POS1 = 56.0

DVE_CMP = {(0, 1), (1, 1), (2, 1)}


def gat_moe_kernel(nc, x, adj, w_seq, a1, a2, w_out, b_out, ln_g, ln_b, attn_w, attn_b, w1, b1,
                   w2, b2, next_w, next_b, out):
    ctx = ExitStack()
    with ctx:
        def sb(name, shape, dt):
            return ctx.enter_context(nc.sbuf_tensor(name, shape, dt))

        def sem(name):
            return ctx.enter_context(nc.semaphore(name))

        def view(region, start, dt, *dims):
            size = {F32: 4, F16: 2, BF16: 2, F8: 1, U8: 1, U32: 4}[dt]
            n = size
            for d in dims:
                n *= d
            ap = region[:, start:start + n].bitcast(dt)
            names = [f"d{i}" for i in range(len(dims))]
            if len(dims) > 1:
                ap = ap.rearrange(f"p ({' '.join(names)}) -> p {' '.join(names)}",
                                  **dict(zip(names[1:], dims[1:])))
            return ap

        region_g = sb("region_g", [P, 65536], U8)
        region_m = sb("region_m", [P, 32768], U8)
        region_s = sb("region_s", [P, T * H * V1 * 4], U8)
        region_w = sb("region_w", [P, 3 * 8192], U8)
        region_x = sb("region_x", [P, 37504], U8)
        region_e = sb("region_e", [P, 8448], U8)
        region_c = sb("region_c", [P, 6144], U8)

        x_all = view(region_g, 0, F32, T, D)
        adj_f = [view(region_g, 32768 + 8192 * u, F32, N) for u in range(2)]
        adj_b = [view(region_g, 49152 + 4096 * u, BF16, N) for u in range(2)]
        wseq_hi = view(region_g, 57344, F16, K, D)
        wseq_lo = view(region_g, 61440, F16, K, D)
        wa_prod = view(region_m, 0, F32, K * H, DH)
        b1_rows = view(region_m, 8192, F32, P)
        vec_rows = view(region_m, 8704, F32, P)
        mask_u8 = view(region_m, 0, U8, T, N)
        mask_f8 = view(region_m, 0, F8, T, N)
        mask_u32 = view(region_m, 0, U32, T, N // 4)
        wseq_f = view(region_x, 0, F32, K, D)
        wother_f = view(region_x, 8192, F32, K * D)
        xn0 = [view(region_x, 16384 + 2048 * u, F32, D) for u in range(2)]
        xnT_hi = [view(region_x, 20480 + 2048 * u, F16, K, P) for u in range(2)]
        xnT_lo = [view(region_x, 21504 + 2048 * u, F16, K, P) for u in range(2)]
        s1T = view(region_x, 24832, F32, N)
        wa_f = view(region_x, 33280, F32, K, 2, H)
        wa_hi = view(region_x, 33792, F16, K, 2 * H)
        wa_lo = view(region_x, 34048, F16, K, 2 * H)
        a_row = view(region_x, 34304, F32, 2, DH)
        s12 = view(region_e, 0, F32, T, 2 * H)
        su = view(region_e, 2048, F32, T, H)
        st_a = view(region_e, 3072, F32, T, H)
        st_c = view(region_e, 4096, F32, T, H)

        g_u8 = [view(region_g, 32768 * b, U8, T, 2, HALF) for b in range(2)]
        g_f8 = [view(region_g, 32768 * b, F8, T, 2, HALF) for b in range(2)]
        g_u32 = [view(region_g, 32768 * b, U32, T, 2, HALF // 4) for b in range(2)]
        seqv = view(region_s, 0, F32, T, H * V1)
        s1_row = [view(region_x, 8192 * b, F32, 2, HALF) for b in range(2)]
        w_att = [view(region_x, 16384 + 8448 * b, F16, T, 2, 4 * V1) for b in range(2)]
        w_prod = view(region_x, 33280, F32, T // 2, 2, 2 * V1)
        acc_lo = [view(region_e, 2112 * g, F32, 4, 2, 2 * V1) for g in range(2)]
        acc_s = [view(region_e, 4224 + 2112 * g, F32, 4, 2, 2 * V1) for g in range(2)]
        thr = view(region_c, 0, F32, PAIRS, 2, T, 2)
        e_b = view(region_c, 2048, F32, T, H)
        e_d = view(region_c, 3072, F32, T, H)
        a_c = view(region_c, 4096, F32, T, H, 2)
        thr_now = [sb(f"thr_now{b}", [P, 2, T, 2], F32) for b in range(2)]

        wpart_hi = [view(region_g, 8192 * c, F16, 4, D) for c in range(8)]
        wpart_lo = [view(region_g, 8192 * c + 4096, F16, 4, D) for c in range(8)]
        h_hi = view(region_m, 0, F16, FT, 256)
        h_lo = view(region_m, 8192, F16, FT, 256)
        parts = [(view(region_m, 16384 + 4096 * i, F16, K, 256),
                  view(region_m, 18432 + 4096 * i, F16, K, 256)) for i in range(4)]
        (hidT_hi, hidT_lo), (xlT_hi, xlT_lo), (xaT_hi, xaT_lo), (yT_hi, yT_lo) = parts
        w_stage = [view(region_x, 8192 * s, F32, 4, D) for s in range(2)]
        hid = view(region_x, 16384, F32, 2, D)
        xl = view(region_x, 20480, F32, K, 256)
        x_res = view(region_x, 20480, F32, 2, D)
        xn = view(region_x, 24576, F32, 2, D)
        h_f = [view(region_x, 28672 + 2048 * i, F32, 2, 256) for i in range(2)]
        y_f = view(region_x, 32768, F32, K, 256)
        y_rows = view(region_x, 32768, F32, 2, D)
        z = view(region_e, 0, F32, 2, D)
        en = view(region_e, 4096, F32, 2, D)
        bout_row, battn_row, bnext_row = [view(region_c, 2048 * i, F32, D) for i in range(3)]
        fixed = [(view(region_w, 8192 * i, F16, K, D), view(region_w, 8192 * i + 4096, F16, K, D))
                 for i in range(3)]
        (wout_hi, wout_lo), (wattn_hi, wattn_lo), (wnext_hi, wnext_lo) = fixed

        ident = sb("ident", [P, P], F32)
        ident_b = sb("ident_b", [P, P], BF16)
        s1_now = [sb(f"s1_now{u}", [P, H], F32) for u in range(2)]
        stats = sb("stats", [P, T, 6], F32)
        mv = sb("mv", [P, T, 2], F32)
        ln_v = sb("ln_v", [P, T], F32)
        minus_half = sb("minus_half", [P, T], F32)
        ln_r = sb("ln_r", [P, T], F32)
        rowsum = sb("rowsum", [P, 2], F32)
        lonely = sb("lonely", [P, 2], F32)
        smax = sb("smax", [P, H], F32)
        smax_all = sb("smax_all", [P, H], F32)
        rden = sb("rden", [P, 2, H], F32)
        b1_col = sb("b1_col", [P, E, FT], F32)
        vec_col = sb("vec_col", [P, VEC], F32)
        b2_col = vec_col[:, 0:E * K].rearrange("p (e k) -> p e k", k=K)
        g_col, b_col = vec_col[:, E * K:E * K + K], vec_col[:, E * K + K:VEC]

        s1T_dram = nc.dram_tensor("s1T_dram", (H, N), F32, kind="Internal").ap()

        ps = ctx.enter_context(nc.psum_tensor("ps", [P, 8, 512], F32))
        ps_adjT = [ps[:, 6 + i, :].bitcast(BF16).rearrange("p (j i) -> p j i", i=P) for i in range(2)]
        ps_tr = ps[:, 0:2, :].rearrange("p b c -> p (b c)").rearrange("p (k c) -> p k c", k=K)
        ps_mm = ps[:, 2:4, :]
        ps_h = [ps[:, 4 + i, :].rearrange("p (f c) -> p f c", f=2) for i in range(2)]
        ps_y = ps[:, 6:8, :].rearrange("p b c -> p (b c)").rearrange("p (k c) -> p k c", k=K)

        x_t = x.rearrange("(t p) d -> p t d", p=P)
        x_e = x.rearrange("(u t p) d -> p u t d", p=P, u=2)
        out_e = out.rearrange("(u t p) d -> p u t d", p=P, u=2)
        adj_t = adj.rearrange("(t p) j -> p t j", p=P)
        w1_c = w1.rearrange("e (k p) (c f) -> p e c k f", p=P, c=4)
        w2_c = w2.rearrange("e (c k p) d -> p e c k d", p=P, c=4)

        x_in = [sem(f"x_in{i}") for i in range(4)]
        wseq_in, a_in, wother_in, cols_in = sem("wseq_in"), sem("a_in"), sem("wother_in"), sem("cols_in")
        adj_in = [sem(f"adj_in{u}") for u in range(2)]
        ident_made, cols_turned, cols_evac = sem("ident_made"), sem("cols_turned"), sem("cols_evac")
        wseq_hi_done, wseq_lo_done, wa_step = sem("wseq_hi_done"), sem("wseq_lo_done"), sem("wa_step")
        wother_step = sem("wother_step")
        ln_step, ln_root = sem("ln_step"), sem("ln_root")
        xn_ready, xT_done, xhi_done, xlo_done = sem("xn_ready"), sem("xT_done"), sem("xhi_done"), sem("xlo_done")
        s_done, seq_done, s_evac, seq_evac = sem("s_done"), sem("seq_done"), sem("s_evac"), sem("seq_evac")
        adj_cast, lonely_done, adj_bin = sem("adj_cast"), sem("lonely_done"), sem("adj_bin")
        adjT_a, adjT_b, mask_dve, mask_act = sem("adjT_a"), sem("adjT_b"), sem("mask_dve"), sem("mask_act")
        sT_done, sT_evac, s1T_out = sem("sT_done"), sem("sT_evac"), sem("s1T_out")
        smax_done, smax_all_done = sem("smax_done"), sem("smax_all_done")
        coef_step, exp_done = sem("coef_step"), sem("exp_done")
        s1_row_in = [sem(f"s1_row_in{b}") for b in range(2)]
        thr_ready, w_prod_step, w_ready = sem("thr_ready"), sem("w_prod_step"), sem("w_ready")
        act_cmp, dve_cmp, g_ready, g_free = sem("act_cmp"), sem("dve_cmp"), sem("g_ready"), sem("g_free")
        acc_done, lo_copied, acc_free = sem("acc_done"), sem("lo_copied"), sem("acc_free")
        acc_scaled, num_done = sem("acc_scaled"), sem("num_done")
        rows_in = sem("rows_in")
        w_in = [sem(f"w_in{s}") for s in range(2)]
        whi_done, wlo_done = sem("whi_done"), sem("wlo_done")
        rden_done, hid_ready, x_res_in = sem("rden_done"), sem("hid_ready"), sem("x_res_in")
        tr_done, tr_hi, tr_free = sem("tr_done"), sem("tr_hi"), sem("tr_free")
        mo_done, mo_free, ma_done, ma_free = sem("mo_done"), sem("mo_free"), sem("ma_done"), sem("ma_free")
        nx_done, nx_free = sem("nx_done"), sem("nx_free")
        z_ready, en_ready, elu_step = sem("z_ready"), sem("en_ready"), sem("elu_step")
        norm_step, norm_root, xh_ready = sem("norm_step"), sem("norm_root"), sem("xh_ready")
        xl_hi_done, xl_lo_done, xa_ready = sem("xl_hi_done"), sem("xl_lo_done"), sem("xa_ready")
        h_done, h_gelu, hhi_done, hlo_done = sem("h_done"), sem("h_gelu"), sem("hhi_done"), sem("hlo_done")
        y_done, y_evac, yhi_done, ylo_done = sem("y_done"), sem("y_evac"), sem("yhi_done"), sem("ylo_done")
        og_ready, out_ready, out_stored = sem("og_ready"), sem("out_ready"), sem("out_stored")

        def settle(eng):
            eng.nop(nofuse=True)

        def wait(eng, semaphore, value):
            if not isinstance(value, int) or value > 0:
                eng.wait_ge(semaphore, value)

        def over_tiles(eng, one, start, stop):
            first, last = 4, T - 2
            for t in range(start, first):
                one(t, t % 2)
            with eng.Fori(first // 2, last // 2) as i:
                one(2 * i, 0)
                one(2 * i + 1, 1)
            for t in range(last, stop):
                one(t, t % 2)

        def is_tile(t):
            return not isinstance(t, int) or 0 <= t < T

        block = ctx.enter_context(nc.Block())

        @block.sync
        def _(sp):
            for i in range(4):
                if i == 1:
                    sp.dma_start(wseq_f, w_seq.rearrange("(k p) n -> p k n", p=P)).then_inc(wseq_in, 16)
                    sp.dma_start(a_row[:, 0, :], a1.partition_broadcast(P)).then_inc(a_in, 16)
                    sp.dma_start(a_row[:, 1, :], a2.partition_broadcast(P)).then_inc(a_in, 16)
                sp.dma_start(x_all[:, 4 * i:4 * i + 4, :], x_t[:, 4 * i:4 * i + 4, :]).then_inc(x_in[i], 16)
            for u in range(2):
                sp.dma_start(adj_f[u], adj_t[:, u, :]).then_inc(adj_in[u], 16)
            with sp.Fori(1, T // 2) as i:
                for u in range(2):
                    sp.wait_ge(adj_cast, 2 * i + u - 1)
                    sp.dma_start(adj_f[u], adj_t[:, 2 * i + u, :]).then_inc(adj_in[u], 16)

            def load_s1_row(q, b):
                sp.dma_start(s1_row[b], s1T_dram[bass.ds(2 * q, 2), b * HALF:(b + 1) * HALF]
                             .partition_broadcast(P)).then_inc(s1_row_in[b], 16)

            sp.wait_ge(s1T_out, 16)
            sp.wait_ge(wother_step, 9)
            for b in range(2):
                load_s1_row(0, b)
            with sp.Fori(1, PAIRS) as q:
                for b in range(2):
                    sp.wait_ge(act_cmp, 16 * q + 8 * b - 8)
                    sp.wait_ge(dve_cmp, 16 * q + 8 * b - 8)
                    load_s1_row(q, b)

            sp.wait_ge(act_cmp, 16 * PAIRS)
            sp.wait_ge(dve_cmp, 16 * PAIRS)

            def load_chunk(e, c, first=False):
                if not first:
                    sp.wait_ge(wlo_done, 8 * e + c - 1)
                src = w1_c[:, e, c] if c < 4 else w2_c[:, e, c - 4]
                sp.dma_start(w_stage[c % 2], src).then_inc(w_in[c % 2], 16)

            for c in range(8):
                load_chunk(0, c, first=(c < 2))
                if c == 5:
                    sp.wait_ge(num_done, 4 * PAIRS)
                    for row, src in ((bout_row, b_out), (battn_row, attn_b), (bnext_row, next_b)):
                        sp.dma_start(row, src.partition_broadcast(P)).then_inc(rows_in, 16)
                    sp.dma_start(x_res, x_e[:, :, 0, :]).then_inc(x_res_in, 16)
            with sp.Fori(1, E) as e:
                for c in range(8):
                    load_chunk(e, c)
                    if c == 0:
                        sp.wait_ge(xl_lo_done, e)
                        sp.dma_start(x_res, x_e[:, :, e, :]).then_inc(x_res_in, 16)

        @block.gpsimd
        def _(pool):
            pool.memset(ident[:, :], 0.0).then_inc(ident_made, 1)
            pool.memset(ident_b[:, :], 0.0).then_inc(ident_made, 1)
            pool.wait_ge(ident_made, 2)
            for m in (ident, ident_b):
                pool.affine_select(out=m[:, :], in_=m[:, :], compare_op=ALU.not_equal, fill=1.0, base=0,
                                   pattern=[[-1, P]], channel_multiplier=1).then_inc(ident_made, 1)
            pool.dma_start(b1_rows, b1.rearrange("e (f p) -> (e f) p", p=P)).then_inc(cols_in, 16)
            pool.dma_start(vec_rows[0:E * K], b2.rearrange("e (k p) -> (e k) p", p=P)).then_inc(cols_in, 16)
            pool.dma_start(vec_rows[E * K:E * K + K], ln_g.rearrange("(k p) -> k p", p=P)).then_inc(cols_in, 16)
            pool.dma_start(vec_rows[E * K + K:VEC], ln_b.rearrange("(k p) -> k p", p=P)).then_inc(cols_in, 16)
            pool.memset(minus_half[:, :], -0.5).then_inc(ident_made, 1)
            pool.wait_ge(ident_made, 5)

            def inverse_root(cols, n, root):
                pool.tensor_scalar(ln_v[:, cols], mv[:, cols, 1], EPS, 1.0, ALU.add, ALU.mult).then_inc(root, 1)
                pool.wait_ge(root, n + 1)
                settle(pool)
                pool.tensor_tensor(ln_r[:, cols], ln_v[:, cols], minus_half[:, cols], ALU.pow).then_inc(root, 1)

            for i in range(4):
                pool.wait_ge(ln_step, 2 * i + 2)
                inverse_root(slice(4 * i, 4 * i + 4), 2 * i, ln_root)
            for i, w in enumerate((w_out, attn_w, next_w)):
                hi, lo = fixed[i]
                flat_hi, flat_lo = (a.rearrange("p k n -> p (k n)") for a in (hi, lo))
                if i:
                    pool.wait_ge(wother_step, 3 * i)
                pool.dma_start(wother_f.rearrange("p (k n) -> p k n", k=K),
                               w.rearrange("(k p) n -> p k n", p=P)).then_inc(wother_in, 16)
                pool.wait_ge(wother_in, 16 * (i + 1))
                pool.tensor_scalar(wother_f, wother_f, WS, 1.0, ALU.mult, ALU.mult).then_inc(wother_step, 1)
                pool.wait_ge(wother_step, 3 * i + 1)
                pool.tensor_copy(flat_hi, wother_f).then_inc(wother_step, 1)
                pool.wait_ge(wother_step, 3 * i + 2)
                pool.tensor_tensor(flat_lo, wother_f, flat_hi, ALU.subtract).then_inc(wother_step, 1)
            pool.wait_ge(sT_evac, T)
            pool.dma_start(s1T_dram, s1T[0:H, :]).then_inc(s1T_out, 16)
            pool.wait_ge(smax_done, 1)
            pool.partition_all_reduce(smax_all[:, :], smax[:, :], P, bass.bass_isa.ReduceOp.max)\
                .then_inc(smax_all_done, 1)

            def step(e, ffn=True, ahead=True):
                if ahead:
                    for norm in range(2):
                        pool.wait_ge(norm_step, 5 * (e + 1) + 2 + 3 * norm)
                        settle(pool)
                        inverse_root(slice(0, 2), 4 * (e + 1) + 2 * norm, norm_root)
                if ffn:
                    pool.wait_ge(out_ready, e + 1)
                    pool.dma_start(out_e[:, :, e, :], y_rows).then_inc(out_stored, 16)

            step(-1, ffn=False)
            step(0)
            with pool.Fori(1, E - 1) as e:
                step(e)
            step(E - 1, ahead=False)
            pool.wait_ge(out_stored, 16 * E)

        @block.tensor
        def _(pe):
            def three(outp, a_hi, a_lo, b_hi, b_lo, start, stop, **kw):
                pe.matmul(outp, a_hi, b_hi, start=start, stop=False, **kw)
                pe.matmul(outp, a_hi, b_lo, start=False, stop=False, **kw)
                return pe.matmul(outp, a_lo, b_hi, start=False, stop=stop, **kw)

            pe.wait_ge(ident_made, 4)
            pe.wait_ge(cols_in, 64)
            pe.transpose(ps[:, 7, 0:P], b1_rows, ident[:, :])
            pe.transpose(ps[:, 7, P:P + VEC], vec_rows[0:VEC], ident[0:VEC, 0:VEC]).then_inc(cols_turned, 1)

            def turn_adjacency(t, u):
                wait(pe, adj_bin, t + 1)
                for half, (read, done) in enumerate(((mask_dve, adjT_a), (mask_act, adjT_b))):
                    wait(pe, read, t)
                    for j in range(8):
                        jj = 8 * half + j
                        last = pe.transpose(ps_adjT[half][:, j, :], adj_b[u][:, jj * P:(jj + 1) * P], ident_b[:, :])
                    last.then_inc(done, 1)

            def turn_rows(t, u):
                wait(pe, xn_ready, t + 1)
                wait(pe, xlo_done, t - 1)
                for k in range(K):
                    last = pe.transpose(ps[:, u, k * P:(k + 1) * P], xn0[u][:, k * P:(k + 1) * P], ident[:, :])
                last.then_inc(xT_done, 1)

            def scores_and_values(t, u):
                wait(pe, xlo_done, t + 1)
                wait(pe, seq_evac, t - 1)
                wait(pe, sT_evac, t - 1)
                for k in range(K):
                    last = three(ps[:, 4 + u, 0:2 * H], xnT_hi[u][:, k], xnT_lo[u][:, k], wa_hi[:, k], wa_lo[:, k],
                                 k == 0, k == K - 1)
                last.then_inc(s_done, 1)
                for k in range(K):
                    last = three(ps[:, 2 + u, :], xnT_hi[u][:, k], xnT_lo[u][:, k], wseq_hi[:, k], wseq_lo[:, k],
                                 k == 0, k == K - 1)
                last.then_inc(seq_done, 1)

            def turn_s1(t, u):
                wait(pe, s_evac, t + 1)
                pe.transpose(ps[0:H, 4 + u, P:2 * P], s1_now[u][:, :], ident[:, :]).then_inc(sT_done, 1)

            def setup(t, u):
                if is_tile(t - 2):
                    turn_s1(t - 2, u)
                if is_tile(t):
                    turn_adjacency(t, u)
                if is_tile(t + 1):
                    turn_rows(t + 1, 1 - u)
                if isinstance(t, int) and t == 0:
                    pe.wait_ge(wseq_lo_done, 1)
                    pe.wait_ge(wa_step, 6)
                if is_tile(t):
                    scores_and_values(t, u)

            pe.wait_ge(cols_evac, 3)
            over_tiles(pe, setup, -1, T + 2)

            def pair(q, wb, first=False):
                w = w_att[wb]
                pe.wait_ge(w_ready, 2 * q + 2)
                for b in range(2):
                    for g in range(2):
                        group = 4 * q + 2 * b + g
                        if not (first and b == 0):
                            pe.wait_ge(acc_free, group - 1)
                        else:
                            pe.wait_ge(mask_act, T)
                            pe.wait_ge(mask_dve, T)
                            pe.wait_ge(coef_step, 9)
                        for c in range(T // 2):
                            if g == 0:
                                pe.wait_ge(g_ready, 16 * q + 8 * b + c + 1)
                            if g == 0 or c == 0:
                                settle(pe)
                            for j in (2 * c, 2 * c + 1):
                                for a in range(4):
                                    acc = ps[:, 4 * g + a, 0:8 * V1]
                                    cols = slice((4 * g + a) * P, (4 * g + a + 1) * P)
                                    for hh in range(2):
                                        last_g = pe.matmul(acc[:, hh * 4 * V1:(hh + 1) * 4 * V1],
                                                           g_f8[b][:, j, hh, cols], w[:, j, hh, :],
                                                           start=(j == 0 and hh == 0), stop=False,
                                                           skip_group_check=True)
                                    rows = slice(b * HALF + (4 * g + a) * P, b * HALF + (4 * g + a + 1) * P)
                                    last_m = pe.matmul(acc.rearrange("p (x k c) -> p x k c", k=2, c=V1)[:, :, 1, :],
                                                       mask_f8[:, j, rows],
                                                       w[:, j].rearrange("p h (x k c) -> p (h x) k c", k=2, c=V1)[:, :, 1, :],
                                                       start=False, stop=(j == T - 1), skip_group_check=True)
                            if g == 1:
                                last_g.then_inc(g_free, 1)
                        last_m.then_inc(acc_done, 1)

            pair(0, 0, first=True)
            pair(1, 1)
            with pe.Fori(0, PAIRS // 2 - 1) as i:
                pair(2 * i + 2, 0)
                pair(2 * i + 3, 1)

            def transpose_rows(src, n, ready, count, first=False):
                pe.wait_ge(ready, count)
                if not first:
                    pe.wait_ge(tr_free, n)
                for k in range(K):
                    for u in range(2):
                        last = pe.transpose(ps_tr[:, k, u * P:(u + 1) * P], src[:, u, k * P:(k + 1) * P], ident[:, :])
                last.then_inc(tr_done, 1)

            def project(a_hi, a_lo, b_hi, b_lo, done):
                for u in range(2):
                    for k in range(K):
                        rows = slice(u * P, (u + 1) * P)
                        last = three(ps_mm[:, u, :], a_hi[:, k, rows], a_lo[:, k, rows], b_hi[:, k], b_lo[:, k],
                                     k == 0, k == K - 1)
                last.then_inc(done, 1)

            def w1_tiles(e, fp, first=False):
                c = fp // 2
                if fp % 2 == 0:
                    pe.wait_ge(wlo_done, 8 * e + c + 1)
                if fp == 0:
                    pe.wait_ge(tr_free, 3 * e + 3)
                if not (first and fp < 2):
                    pe.wait_ge(h_gelu, 8 * e + fp - 1)
                for f in range(2):
                    cols = slice((2 * fp + f) % 4 * P, ((2 * fp + f) % 4 + 1) * P)
                    for k in range(K):
                        last = three(ps_h[fp % 2][:, f, :], wpart_hi[c][:, k, cols], wpart_lo[c][:, k, cols],
                                     xaT_hi[:, k], xaT_lo[:, k], k == 0, k == K - 1)
                last.then_inc(h_done, 1)

            def w2_tiles(e, c, ds, first):
                if ds[0] == 0:
                    pe.wait_ge(wlo_done, 8 * e + c + 5)
                    pe.wait_ge(hlo_done, 8 * e + 2 * c + 2)
                    if c == 0 and not first:
                        pe.wait_ge(y_evac, 2 * e)
                for f in range(4):
                    ft = 4 * c + f
                    for d in ds:
                        last = three(ps_y[:, d, :], wpart_hi[4 + c][:, f, d * P:(d + 1) * P],
                                     wpart_lo[4 + c][:, f, d * P:(d + 1) * P], h_hi[:, ft], h_lo[:, ft],
                                     ft == 0 and d % 2 == 0, ft == FT - 1, skip_group_check=True)
                last.then_inc(y_done, 1)

            def next_rows(e):
                for kk in range(2):
                    pe.wait_ge(ylo_done, 2 * e + kk + 1)
                    for u in range(2):
                        for k in (2 * kk, 2 * kk + 1):
                            rows = slice(u * P, (u + 1) * P)
                            last = three(ps_mm[:, u, :], yT_hi[:, k, rows], yT_lo[:, k, rows], wnext_hi[:, k],
                                         wnext_lo[:, k], k == 0, k == K - 1)
                last.then_inc(nx_done, 1)

            def step(e, ffn=True, ahead=True, first=False):
                n = e + 1
                if ffn:
                    w1_tiles(e, 0, first)
                    w1_tiles(e, 1, first)
                if ahead:
                    transpose_rows(hid, 3 * n, hid_ready, n + 1, first=not ffn)
                if ffn:
                    w1_tiles(e, 2)
                    w1_tiles(e, 3)
                if ahead:
                    pe.wait_ge(tr_free, 3 * n + 1)
                    if ffn and not first:
                        pe.wait_ge(nx_free, e)
                    project(hidT_hi, hidT_lo, wout_hi, wout_lo, mo_done)
                if ffn:
                    for fp in range(4, 8):
                        w1_tiles(e, fp)
                    w2_tiles(e, 0, range(4), first)
                if ahead:
                    transpose_rows(z, 3 * n + 1, xh_ready, n + 1)
                if ffn:
                    w2_tiles(e, 1, range(4), first)
                    w2_tiles(e, 2, range(4), first)
                if ahead:
                    pe.wait_ge(xl_lo_done, n + 1)
                    pe.wait_ge(mo_free, n + 1)
                    project(xlT_hi, xlT_lo, wattn_hi, wattn_lo, ma_done)
                if ffn:
                    w2_tiles(e, 3, range(0, 2), first)
                    w2_tiles(e, 3, range(2, 4), first)
                if ahead:
                    transpose_rows(z, 3 * n + 2, xa_ready, n + 1)
                if ffn:
                    if ahead:
                        pe.wait_ge(ma_free, n + 1)
                    else:
                        pe.wait_ge(nx_free, e)
                    next_rows(e)

            pe.wait_ge(acc_free, 4 * PAIRS)
            pe.wait_ge(wother_step, 9)
            step(-1, ffn=False)
            step(0, first=True)
            with pe.Fori(1, E - 1) as e:
                step(e)
            step(E - 1, ahead=False)

        @block.scalar
        def _(act):
            act.wait_ge(wseq_in, 16)
            act.activation(wseq_hi, wseq_f, ACT.Copy, scale=WS).then_inc(wseq_hi_done, 1)

            def cast(t, u):
                wait(act, adj_in[u], 16 * (t // 2 + 1) if isinstance(t, int) else 8 * (t - u) + 16)
                wait(act, adjT_b, t - 1)
                act.activation(adj_b[u], adj_f[u], ACT.Copy, accum_out=rowsum[:, u:u + 1]).then_inc(adj_cast, 1)

            def high_rows(t, u):
                wait(act, xT_done, t + 1)
                wait(act, seq_done, t - 1)
                act.activation(xnT_hi[u].rearrange("p k c -> p (k c)"), ps[:, u, :], ACT.Copy, scale=XS)\
                    .then_inc(xhi_done, 1)

            def setup(t, u):
                if is_tile(t - 2):
                    wait(act, sT_done, t - 1)
                    act.activation(s1T[0:H, bass.ds((t - 2) * P, P)], ps[0:H, 4 + u, P:2 * P], ACT.Copy)\
                        .then_inc(sT_evac, 1)
                if is_tile(t + 1):
                    high_rows(t + 1, 1 - u)
                if is_tile(t + 2):
                    cast(t + 2, u)
                if is_tile(t):
                    wait(act, adjT_b, t + 1)
                    act.activation(mask_u8[:, 8:16, bass.ds(t * P, P)], ps_adjT[1], ACT.Copy, scale=NEG1)\
                        .then_inc(mask_act, 1)

            over_tiles(act, setup, -2, T + 2)

            act.wait_ge(coef_step, 3)
            act.activation(e_b, su, ACT.Exp).then_inc(exp_done, 1)
            act.activation(e_d, su, ACT.Exp, scale=0.2).then_inc(exp_done, 1)
            act.wait_ge(coef_step, 6)
            act.activation(a_c[:, :, :, 0], st_a, ACT.Exp).then_inc(exp_done, 1)
            act.activation(a_c[:, :, :, 1], st_c, ACT.Exp).then_inc(exp_done, 1)

            def copy_low(q, b, g):
                group = 4 * q + 2 * b + g
                act.wait_ge(acc_done, group + 1)
                act.activation(acc_lo[g], ps[:, 4 * g:4 * g + 4, 0:8 * V1]
                               .rearrange("p a (h x c) -> p a h x c", h=2, x=2)[:, :, :, 1, :], ACT.Copy)\
                    .then_inc(lo_copied, 1)

            def compare_unit(q, b, tb, evac, free):
                act.wait_ge(s1_row_in[b], 16 * (q + 1))
                for c in range(T // 2):
                    if evac and c in (0, 4):
                        copy_low(q - 1, b, c // 4)
                    if free:
                        act.wait_ge(g_free, 16 * (q - 1) + 8 * b + c + 1)
                    if free or c == 0:
                        settle(act)
                    for j in (2 * c, 2 * c + 1):
                        for hh in range(2):
                            if (j % 4, hh) not in DVE_CMP:
                                last = act.activation(g_f8[b][:, j, hh, :], s1_row[b][:, hh, :], ACT.Sigmoid,
                                                      bias=thr_now[tb][:, 1, j, hh:hh + 1], scale=BIG,
                                                      saturate=False)
                    last.then_inc(act_cmp, 1)

            def pair(q, tb, evac=True):
                act.wait_ge(thr_ready, q + 1)
                for b in range(2):
                    compare_unit(q, b, tb, evac, evac)

            act.wait_ge(adjT_b, T)
            pair(0, 0, evac=False)
            pair(1, 1)
            with act.Fori(0, PAIRS // 2 - 1) as i:
                pair(2 * i + 2, 0)
                pair(2 * i + 3, 1)
            def split_chunk(e, c, first=False):
                act.wait_ge(w_in[c % 2], 16 * (4 * e + c // 2 + 1))
                if first:
                    act.wait_ge(acc_done, 4 * PAIRS - 2 if c < 4 else 4 * PAIRS)
                elif c < 4:
                    act.wait_ge(h_done, 8 * (e - 1) + 2 * c + 2)
                else:
                    act.wait_ge(y_done, 5 * (e - 1) + (c - 3 if c < 7 else 5))
                act.activation(wpart_hi[c], w_stage[c % 2], ACT.Copy, scale=WS).then_inc(whi_done, 1)

            def transposed_hi(dst, n):
                act.wait_ge(tr_done, n + 1)
                act.activation(dst, ps_tr, ACT.Copy, scale=XS).then_inc(tr_hi, 1)

            def gelu(e, fp, first=False):
                act.wait_ge(h_done, 8 * e + fp + 1)
                if not (first and fp < 2):
                    act.wait_ge(hlo_done, 8 * e + fp - 1)
                for f in range(2):
                    bias = b1_col[:, bass.ds(e, 1), 2 * fp + f:2 * fp + f + 1].rearrange("p a b -> p (a b)")
                    last = act.activation(h_f[fp % 2][:, f, :], ps_h[fp % 2][:, f, :], ACT.Gelu,
                                          bias=bias, scale=1.0 / (WS * XS))
                last.then_inc(h_gelu, 1)

            def step(e, ffn=True, ahead=True, first=False):
                n = e + 1
                if ffn:
                    gelu(e, 0, first)
                    gelu(e, 1, first)
                if ahead:
                    transposed_hi(hidT_hi, 3 * n)
                    if ffn:
                        split_chunk(n, 0)
                if ffn:
                    gelu(e, 2)
                    gelu(e, 3)
                if ahead:
                    if ffn:
                        split_chunk(n, 1)
                    act.wait_ge(z_ready, n + 1)
                    act.activation(en, z, ACT.Exp).then_inc(en_ready, 1)
                if ffn:
                    gelu(e, 4)
                    gelu(e, 5)
                    if ahead:
                        split_chunk(n, 2)
                    gelu(e, 6)
                    gelu(e, 7)
                    if ahead:
                        split_chunk(n, 3)
                elif ahead:
                    for c in range(4, 7):
                        split_chunk(n, c, first=True)
                if ahead:
                    act.wait_ge(tr_free, 3 * n + 2)
                    act.activation(xlT_hi, xl, ACT.Copy, scale=XS).then_inc(xl_hi_done, 1)
                    if ffn:
                        for c in range(4, 7):
                            split_chunk(n, c)
                    transposed_hi(xaT_hi, 3 * n + 2)
                    split_chunk(n, 7, not ffn)
                if ffn:
                    act.wait_ge(nx_free, e + 1)
                    act.activation(y_rows, y_rows, ACT.Gelu).then_inc(og_ready, 1)

            act.wait_ge(cols_evac, 3)
            copy_low(PAIRS - 1, 0, 0)
            copy_low(PAIRS - 1, 0, 1)
            for c in range(4):
                split_chunk(0, c, first=True)
            copy_low(PAIRS - 1, 1, 0)
            copy_low(PAIRS - 1, 1, 1)
            step(-1, ffn=False)
            step(0, first=True)
            with act.Fori(1, E - 1) as e:
                step(e)
            step(E - 1, ahead=False)

        @block.vector
        def _(dve):
            for i in range(4):
                dve.wait_ge(x_in[i], 16)
                for t in range(4 * i, 4 * i + 4):
                    last = dve.bn_stats(stats[:, t, :], x_all[:, t, :])
                last.then_inc(ln_step, 1)
                dve.wait_ge(ln_step, 2 * i + 1)
                for t in range(4 * i, 4 * i + 4):
                    last = dve.bn_aggr(mv[:, t, :], stats[:, t, :])
                last.then_inc(ln_step, 1)
            dve.wait_ge(wseq_hi_done, 1)
            dve.scalar_tensor_tensor(wseq_lo, wseq_f, WS, wseq_hi, ALU.mult, ALU.subtract).then_inc(wseq_lo_done, 1)
            dve.wait_ge(a_in, 32)
            for i in range(2):
                dve.tensor_tensor(wa_prod, wseq_f.rearrange("p k (h c) -> p (k h) c", c=DH),
                                  a_row[:, i:i + 1, :].to_broadcast([P, K * H, DH]), ALU.mult).then_inc(wa_step, 1)
                dve.wait_ge(wa_step, 2 * i + 1)
                dve.tensor_reduce(wa_f[:, :, i, :], wa_prod.rearrange("p (k h) c -> p k h c", h=H), AX.X, ALU.add)\
                    .then_inc(wa_step, 1)
                dve.wait_ge(wa_step, 2 * i + 2)
            wa_flat, wah_flat, wal_flat = (wa_f.rearrange("p k i h -> p (k i h)"),
                                           wa_hi.rearrange("p k c -> p (k c)"), wa_lo.rearrange("p k c -> p (k c)"))
            dve.tensor_scalar(wah_flat, wa_flat, WS, None, ALU.mult).then_inc(wa_step, 1)
            dve.wait_ge(wa_step, 5)
            dve.scalar_tensor_tensor(wal_flat, wa_flat, WS, wah_flat, ALU.mult, ALU.subtract).then_inc(wa_step, 1)
            dve.memset(seqv[:, :, DH::V1], 1.0)
            dve.wait_ge(cols_turned, 1)
            dve.tensor_copy(b1_col[:, :, :].rearrange("p e f -> p (e f)"), ps[:, 7, 0:P]).then_inc(cols_evac, 1)
            dve.tensor_scalar(vec_col[:, 0:E * K], ps[:, 7, P:P + E * K], HS, None, ALU.mult).then_inc(cols_evac, 1)
            dve.tensor_copy(vec_col[:, E * K:VEC], ps[:, 7, P + E * K:P + VEC]).then_inc(cols_evac, 1)

            def normal_rows(t, u):
                if isinstance(t, int) and t == 0:
                    dve.wait_ge(ln_root, 8)
                wait(dve, xT_done, t - 1)
                mean = mv[:, bass.ds(t, 1), 0:1].rearrange("p a b -> p (a b)")
                dve.tensor_scalar(xn0[u], x_all[:, bass.ds(t, 1), :].rearrange("p t d -> p (t d)"), mean,
                                  ln_r[:, bass.ds(t, 1)], ALU.subtract, ALU.mult).then_inc(xn_ready, 1)

            def setup(t, u):
                if is_tile(t + 2):
                    normal_rows(t + 2, u)
                if is_tile(t + 1):
                    wait(dve, adj_cast, t + 2)
                    dve.tensor_scalar(lonely[:, 1 - u:2 - u], rowsum[:, 1 - u:2 - u], 0.5, None, ALU.is_lt)\
                        .then_inc(lonely_done, 1)
                if is_tile(t):
                    wait(dve, adjT_a, t + 1)
                    dve.tensor_scalar(mask_u8[:, 0:8, bass.ds(t * P, P)], ps_adjT[0], NEG1, None, ALU.mult)\
                        .then_inc(mask_dve, 1)
                if is_tile(t + 1):
                    wait(dve, lonely_done, t + 2)
                    dve.tensor_scalar(adj_b[1 - u], adj_b[1 - u], lonely[:, 1 - u:2 - u], None, ALU.max)\
                        .then_inc(adj_bin, 1)
                    wait(dve, xhi_done, t + 2)
                    wait(dve, seq_done, t)
                    dve.scalar_tensor_tensor(xnT_lo[1 - u].rearrange("p k c -> p (k c)"), ps[:, 1 - u, :], XS,
                                             xnT_hi[1 - u].rearrange("p k c -> p (k c)"), ALU.mult, ALU.subtract)\
                        .then_inc(xlo_done, 1)
                if is_tile(t - 1):
                    wait(dve, s_done, t)
                    wait(dve, sT_done, t - 2)
                    dve.tensor_scalar(s1_now[1 - u][:, :], ps[:, 5 - u, 0:H], 1.0 / (WS * XS), None, ALU.mult)
                    dve.tensor_scalar(s12[:, bass.ds(t - 1, 1), :].rearrange("p t h -> p (t h)"),
                                      ps[:, 5 - u, 0:2 * H], 1.0 / (WS * XS), None, ALU.mult).then_inc(s_evac, 1)
                    wait(dve, seq_done, t)
                    dve.tensor_scalar(seqv[:, bass.ds(t - 1, 1), :].rearrange("p t (h c) -> p (t h) c", c=V1)[:, :, 0:DH],
                                      ps[:, 3 - u, :].rearrange("p (h c) -> p h c", c=DH),
                                      1.0 / (WS * XS), None, ALU.mult).then_inc(seq_evac, 1)

            over_tiles(dve, setup, -2, T + 1)

            dve.wait_ge(s_evac, T)
            s1, s2 = s12[:, :, 0:H], s12[:, :, H:2 * H]
            dve.tensor_reduce(smax[:, :], s2.rearrange("p t h -> p h t"), AX.X, ALU.max).then_inc(smax_done, 1)
            by_pair = s2.rearrange("p t (q h) -> p t q h", h=2)
            for kind, factor in ((0, -1.0), (1, BIG)):
                dve.tensor_scalar(thr[:, :, kind].rearrange("p q t h -> p t q h"), by_pair, factor, None, ALU.mult)\
                    .then_inc(coef_step, 1)
            dve.wait_ge(smax_all_done, 1)
            top = smax_all[:, :].unsqueeze(1).to_broadcast([P, T, H])
            dve.tensor_tensor(su, s2, top, ALU.subtract).then_inc(coef_step, 1)
            dve.tensor_tensor(st_a, s1, top, ALU.add).then_inc(coef_step, 1)
            dve.wait_ge(coef_step, 4)
            dve.tensor_scalar(st_c, st_a, -0.8, 0.0, ALU.mult, ALU.min).then_inc(coef_step, 1)
            dve.wait_ge(coef_step, 5)
            dve.tensor_scalar(st_a, st_a, 0.8, 0.0, ALU.mult, ALU.min).then_inc(coef_step, 1)
            dve.wait_ge(exp_done, 2)
            dve.tensor_scalar(e_b, e_b, KAPPA, None, ALU.mult).then_inc(coef_step, 1)
            dve.tensor_scalar(e_d, e_d, -KAPPA, None, ALU.mult).then_inc(coef_step, 1)
            dve.wait_ge(seq_evac, T)
            dve.wait_ge(coef_step, 8)
            dve.wait_ge(exp_done, 4)
            dve.tensor_copy(rden[:, :, :], s12[:, 0:2, 0:H]).then_inc(coef_step, 1)

            def make_w(q, wb, first=False):
                dve.tensor_copy(thr_now[wb][:, :, :, :].rearrange("p k t h -> p (k t h)"),
                                thr[:, bass.ds(q, 1)].rearrange("p q k t h -> p (q k t h)")).then_inc(thr_ready, 1)
                for jb in range(2):
                    js = slice(8 * jb, 8 * jb + 8)
                    if not first or jb:
                        dve.wait_ge(w_ready, 2 * q + jb)
                    v = seqv[:, js, bass.ds(2 * q * V1, 2 * V1)].rearrange("p t (h c) -> p t h c", c=V1)
                    for kind, coef in ((0, e_b), (1, e_d)):
                        f = coef[:, js, bass.ds(2 * q, 2)].unsqueeze(3).to_broadcast([P, 8, 2, V1])
                        dve.tensor_tensor(w_prod[:, :, :, kind * V1:(kind + 1) * V1], v, f, ALU.mult)\
                            .then_inc(w_prod_step, 1)
                    dve.wait_ge(w_prod_step, 6 * q + 3 * jb + 2)
                    hi, lo = w_att[wb][:, js, :, 0:2 * V1], w_att[wb][:, js, :, 2 * V1:4 * V1]
                    dve.tensor_copy(hi, w_prod).then_inc(w_prod_step, 1)
                    dve.wait_ge(w_prod_step, 6 * q + 3 * jb + 3)
                    dve.tensor_tensor(lo, w_prod, hi, ALU.subtract).then_inc(w_ready, 1)

            def acc_add(q, b, g):
                group = 4 * q + 2 * b + g
                dve.wait_ge(lo_copied, group + 1)
                dve.tensor_tensor(acc_s[g], ps[:, 4 * g:4 * g + 4, 0:8 * V1]
                                  .rearrange("p a (h x c) -> p a h x c", h=2, x=2)[:, :, :, 0, :],
                                  acc_lo[g], ALU.add).then_inc(acc_free, 1)

            def acc_scale(q, b, g):
                group = 4 * q + 2 * b + g
                dve.wait_ge(acc_free, group + 1)
                s = acc_s[g].rearrange("p a h (k c) -> p a (h k) c", c=V1)
                t0 = 8 * b + 4 * g
                coef = a_c[:, t0:t0 + 4].rearrange("p t h k -> p t (h k)")[:, :, bass.ds(4 * q, 4)]
                dve.tensor_tensor(s, s, coef.unsqueeze(3).to_broadcast([P, 4, 4, V1]), ALU.mult)\
                    .then_inc(acc_scaled, 1)

            def acc_sum(q, b, g):
                group = 4 * q + 2 * b + g
                dve.wait_ge(acc_scaled, group + 1)
                t0 = 8 * b + 4 * g
                dst = seqv[:, t0:t0 + 4, bass.ds(2 * q * V1, 2 * V1)].rearrange("p t (h c) -> p t h c", c=V1)
                dve.tensor_tensor(dst, acc_s[g][:, :, :, 0:V1], acc_s[g][:, :, :, V1:2 * V1], ALU.add)\
                    .then_inc(num_done, 1)

            def mask_chunk(q, b, c):
                dve.wait_ge(act_cmp, 16 * q + 8 * b + c + 1)
                dve.wait_ge(dve_cmp, 16 * q + 8 * b + c + 1)
                g = g_u32[b][:, 2 * c:2 * c + 2]
                m = mask_u32[:, 2 * c:2 * c + 2, b * HALF // 4:(b + 1) * HALF // 4]
                dve.tensor_tensor(g, g, m.unsqueeze(2).to_broadcast([P, 2, 2, HALF // 4]), ALU.bitwise_and)\
                    .then_inc(g_ready, 1)

            def unit(q, b, tb, evac):
                dve.wait_ge(s1_row_in[b], 16 * (q + 1))
                for c in range(T // 2):
                    if evac and c % 4 < 3:
                        (acc_add, acc_scale, acc_sum)[c % 4](q - 1, b, c // 4)
                    if evac:
                        dve.wait_ge(g_free, 16 * (q - 1) + 8 * b + c + 1)
                    for j in (2 * c, 2 * c + 1):
                        for hh in range(2):
                            if (j % 4, hh) in DVE_CMP:
                                last = dve.tensor_scalar(g_u8[b][:, j, hh, :], s1_row[b][:, hh, :],
                                                         thr_now[tb][:, 0, j, hh:hh + 1], POS1, ALU.is_gt, ALU.mult)
                    last.then_inc(dve_cmp, 1)
                    if c:
                        mask_chunk(q, b, c - 1)
                mask_chunk(q, b, T // 2 - 1)

            def pair(q, wb, evac=True):
                make_w(q, wb, first=not evac)
                for b in range(2):
                    unit(q, b, wb, evac)

            dve.wait_ge(mask_act, T)
            dve.wait_ge(mask_dve, T)
            pair(0, 0, evac=False)
            pair(1, 1)
            with dve.Fori(0, PAIRS // 2 - 1) as i:
                pair(2 * i + 2, 0)
                pair(2 * i + 3, 1)
            rows = seqv.rearrange("p (u t) c -> p u t c", u=2)

            def tiles(e, n=H * V1):
                return rows[:, :, bass.ds(e, 1), 0:n].rearrange("p u t c -> p u (t c)")

            def split_chunk(n, c):
                dve.wait_ge(whi_done, 8 * n + c + 1)
                dve.scalar_tensor_tensor(wpart_lo[c], w_stage[c % 2], WS, wpart_hi[c], ALU.mult, ALU.subtract)\
                    .then_inc(wlo_done, 1)

            def transposed_lo(dst, hi, n):
                flat = "p k c -> p (k c)"
                dve.wait_ge(tr_hi, n)
                dve.scalar_tensor_tensor(dst.rearrange(flat), ps_tr.rearrange(flat), XS, hi.rearrange(flat),
                                         ALU.mult, ALU.subtract).then_inc(tr_free, 1)

            def hidden(e):
                num = tiles(e).rearrange("p u (h c) -> p u h c", c=V1)
                dve.reciprocal(rden[:, :, :], num[:, :, :, DH]).then_inc(rden_done, 1)
                dve.wait_ge(rden_done, e + 1)
                dve.tensor_tensor(hid.rearrange("p u (h c) -> p u h c", c=DH), num[:, :, :, 0:DH],
                                  rden[:, :, :].unsqueeze(3).to_broadcast([P, 2, H, DH]), ALU.mult)\
                    .then_inc(hid_ready, 1)

            def elu_in(e):
                dve.wait_ge(mo_done, e + 1)
                dve.scalar_tensor_tensor(z, ps_mm, 1.0 / (WS * XS), bout_row.unsqueeze(1).to_broadcast([P, 2, D]),
                                         ALU.mult, ALU.add).then_inc(mo_free, 1)
                dve.wait_ge(mo_free, e + 1)
                dve.tensor_scalar(xn, z, 0.0, None, ALU.max).then_inc(z_ready, 1)

            def elu_out(e):
                dve.wait_ge(en_ready, e + 1)
                dve.scalar_tensor_tensor(z, en, 1.0, xn, ALU.min, ALU.add).then_inc(elu_step, 1)
                dve.wait_ge(elu_step, 2 * e + 1)
                dve.wait_ge(x_res_in, 16 * (e + 1))
                x1 = tiles(e, D)
                dve.scalar_tensor_tensor(x1, z, -1.0, x_res, ALU.add, ALU.add).then_inc(elu_step, 1)
                dve.wait_ge(elu_step, 2 * e + 2)
                statistics(x1, 5 * e)

            def statistics(src, at):
                settle(dve)
                for u in range(2):
                    last = dve.bn_stats(stats[:, u, :], src[:, u, :])
                last.then_inc(norm_step, 1)
                dve.wait_ge(norm_step, at + 1)
                settle(dve)
                for u in range(2):
                    last = dve.bn_aggr(mv[:, u, :], stats[:, u, :])
                last.then_inc(norm_step, 1)

            def normalise(dst, src, root_at):
                dve.wait_ge(norm_root, root_at)
                for u in range(2):
                    last = dve.tensor_scalar(dst[:, u, :], src[:, u, :], mv[:, u, 0:1], ln_r[:, u:u + 1],
                                             ALU.subtract, ALU.mult)
                return last

            def norm_1(e):
                normalise(xn, tiles(e, D), 4 * e + 2).then_inc(norm_step, 1)
                dve.wait_ge(norm_step, 5 * e + 3)
                statistics(xn, 5 * e + 3)

            def norm_2(e):
                normalise(z, xn, 4 * e + 4).then_inc(xh_ready, 1)

            def gain(e):
                dve.wait_ge(tr_done, 3 * e + 2)
                for k in range(K):
                    last = dve.tensor_scalar(xl[:, k, :], ps_tr[:, k, :], g_col[:, k:k + 1], b_col[:, k:k + 1],
                                             ALU.mult, ALU.add)
                last.then_inc(tr_free, 1)

            def gain_lo(e):
                dve.wait_ge(xl_hi_done, e + 1)
                dve.scalar_tensor_tensor(xlT_lo, xl, XS, xlT_hi, ALU.mult, ALU.subtract).then_inc(xl_lo_done, 1)

            def dense_out(e):
                dve.wait_ge(ma_done, e + 1)
                dve.scalar_tensor_tensor(z, ps_mm, 1.0 / (WS * XS), battn_row.unsqueeze(1).to_broadcast([P, 2, D]),
                                         ALU.mult, ALU.add).then_inc(ma_free, 1)
                dve.wait_ge(ma_free, e + 1)
                dve.tensor_tensor(z, z, xn, ALU.add).then_inc(xa_ready, 1)

            def split_h(e, fp, first):
                dve.wait_ge(h_gelu, 8 * e + fp + 1)
                if not first:
                    dve.wait_ge(y_done, 5 * e)
                pair_of = slice(2 * fp, 2 * fp + 2)
                dve.tensor_scalar(h_hi[:, pair_of], h_f[fp % 2], HS, None, ALU.mult).then_inc(hhi_done, 1)
                dve.wait_ge(hhi_done, 8 * e + fp + 1)
                dve.scalar_tensor_tensor(h_lo[:, pair_of], h_f[fp % 2], HS, h_hi[:, pair_of],
                                         ALU.mult, ALU.subtract).then_inc(hlo_done, 1)

            def y_out(e, kk, first):
                dve.wait_ge(y_done, 5 * e + 4 + kk)
                if not kk and not first:
                    dve.wait_ge(out_stored, 16 * e)
                ks = slice(2 * kk, 2 * kk + 2)
                for k in (2 * kk, 2 * kk + 1):
                    bias = b2_col[:, bass.ds(e, 1), k:k + 1].rearrange("p a b -> p (a b)")
                    last = dve.tensor_scalar(y_f[:, k, :], ps_y[:, k, :], 1.0 / WS, bias, ALU.mult, ALU.add)
                last.then_inc(y_evac, 1)
                dve.wait_ge(y_evac, 2 * e + kk + 1)
                dve.tensor_copy(yT_hi[:, ks], y_f[:, ks]).then_inc(yhi_done, 1)
                dve.wait_ge(yhi_done, 2 * e + kk + 1)
                dve.tensor_tensor(yT_lo[:, ks], y_f[:, ks], yT_hi[:, ks], ALU.subtract).then_inc(ylo_done, 1)

            def next_out(e):
                dve.wait_ge(nx_done, e + 1)
                dve.scalar_tensor_tensor(y_rows, ps_mm, 1.0 / (WS * HS), bnext_row.unsqueeze(1).to_broadcast([P, 2, D]),
                                         ALU.mult, ALU.add).then_inc(nx_free, 1)

            def residual_out(e):
                dve.wait_ge(og_ready, e + 1)
                dve.tensor_tensor(y_rows, y_rows, tiles(e, D), ALU.add).then_inc(out_ready, 1)

            def step(e, ffn=True, ahead=True, first=False):
                n = e + 1
                if ahead and ffn:
                    hidden(n)
                if ffn:
                    split_h(e, 0, first)
                    split_h(e, 1, first)
                if ahead:
                    transposed_lo(hidT_lo, hidT_hi, 2 * n + 1)
                    if ffn:
                        split_chunk(n, 0)
                if ffn:
                    split_h(e, 2, first)
                    split_h(e, 3, first)
                if ahead:
                    if ffn:
                        split_chunk(n, 1)
                    elu_in(n)
                if ffn:
                    split_h(e, 4, first)
                if ahead:
                    elu_out(n)
                if ffn:
                    split_h(e, 5, first)
                    if ahead:
                        split_chunk(n, 2)
                elif ahead:
                    split_chunk(n, 4)
                if ahead:
                    norm_1(n)
                if ffn:
                    split_h(e, 6, first)
                elif ahead:
                    split_chunk(n, 5)
                if ahead:
                    norm_2(n)
                if ffn:
                    split_h(e, 7, first)
                    if ahead:
                        split_chunk(n, 3)
                elif ahead:
                    split_chunk(n, 6)
                if ahead:
                    gain(n)
                    gain_lo(n)
                    if ffn:
                        split_chunk(n, 4)
                        split_chunk(n, 5)
                    dense_out(n)
                    if ffn:
                        split_chunk(n, 6)
                if ffn:
                    y_out(e, 0, first)
                    y_out(e, 1, first)
                if ahead:
                    transposed_lo(xaT_lo, xaT_hi, 2 * n + 2)
                    split_chunk(n, 7)
                if ffn:
                    next_out(e)
                    residual_out(e)

            def last_sum(b, g):
                acc_add(PAIRS - 1, b, g)
                acc_scale(PAIRS - 1, b, g)
                acc_sum(PAIRS - 1, b, g)

            last_sum(0, 0)
            last_sum(0, 1)
            for c in range(4):
                split_chunk(0, c)
            last_sum(1, 0)
            dve.wait_ge(num_done, 4 * PAIRS - 1)
            hidden(0)
            last_sum(1, 1)
            dve.wait_ge(rows_in, 48)
            step(-1, ffn=False)
            step(0, first=True)
            with dve.Fori(1, E - 1) as e:
                step(e)
            step(E - 1, ahead=False)


_USED = ["x", "adj", "L0_gnn_W_seq", "L0_gnn_a1", "L0_gnn_a2", "L0_gnn_W_out", "L0_gnn_b_out",
         "L0_ffn_ln_g", "L0_ffn_ln_b", "L0_ffn_attn_w", "L0_ffn_attn_b", "L0_ffn_w1", "L0_ffn_b1",
         "L0_ffn_w2", "L0_ffn_b2", "L0_ffn_next_w", "L0_ffn_next_b"]


def kernel(**inputs):
    import numpy as _np
    import concourse.bacc as _bacc
    from concourse.bass_utils import run_bass_kernel_spmd as _run

    nc = _bacc.Bacc("TRN2", target_bir_lowering=False, num_devices=1)
    arrays, args = {}, []
    for name in _USED:
        a = _np.ascontiguousarray(inputs[name])
        arrays[f"in_{name}"] = a
        args.append(nc.dram_tensor(f"in_{name}", a.shape, mybir.dt.from_np(a.dtype), kind="ExternalInput").ap())
    out = nc.dram_tensor("out_rows", (N, D), F32, kind="ExternalOutput").ap()
    gat_moe_kernel(nc, *args, out)
    r = _run(nc, [arrays], core_ids=[0])
    return r.results[0]["out_rows"]
```

```python
from contextlib import ExitStack

import concourse.bass as bass
from concourse import mybir

F32 = mybir.dt.float32
F16 = mybir.dt.float16
BF16 = mybir.dt.bfloat16
F8 = mybir.dt.float8e4
U8 = mybir.dt.uint8
U32 = mybir.dt.uint32
ALU = mybir.AluOpType
ACT = mybir.ActivationFunctionType
AX = mybir.AxisListType

P = 128
N = 2048
D = 512
H = 16
DH = D // H
V1 = DH + 1
T = N // P
K = D // P
E = 8
F = 2048
FT = F // P
HALF = N // 2
PAIRS = H // 2
LAG = 4
VEC = E * K + 2 * K
EPS = 1e-5

WS = 2.0 ** 10
XS = 2.0 ** 8
HS = 2.0 ** 6
KAPPA = 2.0 ** 10
BIG = 2.0 ** 100
NEG1 = 184.0
POS1 = 56.0

DVE_CMP = {(b, j, 1) for b in range(2) for j in range(T) if j % 4 < 3} - {(1, 13, 1)}


def gat_moe_kernel(nc, x, adj, w_seq, a1, a2, w_out, b_out, ln_g, ln_b, attn_w, attn_b, w1, b1,
                   w2, b2, next_w, next_b, out):
    ctx = ExitStack()
    with ctx:
        def sb(name, shape, dt):
            return ctx.enter_context(nc.sbuf_tensor(name, shape, dt))

        def sem(name):
            return ctx.enter_context(nc.semaphore(name))

        def view(region, start, dt, *dims):
            size = {F32: 4, F16: 2, BF16: 2, F8: 1, U8: 1, U32: 4}[dt]
            n = size
            for d in dims:
                n *= d
            ap = region[:, start:start + n].bitcast(dt)
            names = [f"d{i}" for i in range(len(dims))]
            if len(dims) > 1:
                ap = ap.rearrange(f"p ({' '.join(names)}) -> p {' '.join(names)}",
                                  **dict(zip(names[1:], dims[1:])))
            return ap

        region_g = sb("region_g", [P, 65536], U8)
        region_m = sb("region_m", [P, 32768], U8)
        region_s = sb("region_s", [P, T * H * V1 * 4], U8)
        region_w = sb("region_w", [P, 3 * 8192], U8)
        region_x = sb("region_x", [P, 37504], U8)
        region_e = sb("region_e", [P, 8448], U8)
        region_c = sb("region_c", [P, 7168], U8)

        x_all = view(region_g, 0, F32, T, D)
        adj_f = [view(region_g, 32768 + 8192 * u, F32, N) for u in range(2)]
        adj_b = [view(region_g, 49152 + 4096 * u, BF16, N) for u in range(2)]
        wseq_hi = view(region_g, 57344, F16, K, D)
        wseq_lo = view(region_g, 61440, F16, K, D)
        wseq_T = view(region_m, 0, F32, K, D)
        b1_rows = view(region_m, 8192, F32, P)
        vec_rows = view(region_m, 8704, F32, P)
        mask_u8 = view(region_m, 0, U8, T, N)
        mask_f8 = view(region_m, 0, F8, T, N)
        mask_u32 = view(region_m, 0, U32, T, N // 4)
        wseq_f = view(region_x, 0, F32, K, D)
        wother_f = view(region_x, 8192, F32, K * D)
        xn0 = [view(region_x, 16384 + 2048 * u, F32, D) for u in range(2)]
        xnT_hi = [view(region_x, 20480 + 2048 * u, F16, K, P) for u in range(2)]
        xnT_lo = [view(region_x, 21504 + 2048 * u, F16, K, P) for u in range(2)]
        s1T = view(region_x, 29056, F32, N)
        a_prod = view(region_x, 24832, F32, P // DH, DH)
        wa_hi = view(region_x, 25344, F16, K, 2 * H)
        wa_lo = view(region_x, 25600, F16, K, 2 * H)
        a_row = view(region_x, 25856, F32, 2, DH)
        a_blocks = view(region_x, 26240, F32, 2, P // DH)
        s1_now = [view(region_x, 26112 + 64 * u, F32, H) for u in range(2)]
        s12 = view(region_e, 0, F32, T, 2 * H)
        su = view(region_e, 2048, F32, T, H)
        st_c = view(region_e, 3072, F32, T, H)

        g_u8 = [view(region_g, 32768 * b, U8, T, 2, HALF) for b in range(2)]
        g_f8 = [view(region_g, 32768 * b, F8, T, 2, HALF) for b in range(2)]
        g_u32 = [view(region_g, 32768 * b, U32, T, 2, HALF // 4) for b in range(2)]
        seqv = view(region_s, 0, F32, T, H * V1)
        s1_row = [view(region_x, 8192 * b, F32, 2, HALF) for b in range(2)]
        w_att = [view(region_x, 16384 + 12672 * b, F16, T, 2, 4 * V1) for b in range(2)]
        w_prod = view(region_x, 24832, F32, T // 2, 2, 2 * V1)
        acc_lo = [view(region_e, 4224 * g, F32, 4, 2, 2 * V1) for g in range(2)]
        acc_s = [view(region_e, 4224 * g + 2112, F32, 4, 2, 2 * V1) for g in range(2)]
        thr = view(region_c, 0, F32, PAIRS, 2, T, 2)
        e_b = view(region_c, 2048, F32, T, H)
        e_d = view(region_c, 3072, F32, T, H)
        c_row = view(region_c, 4096, F32, T, H)
        thr_now = [sb(f"thr_now{b}", [P, 2, T, 2], F32) for b in range(2)]

        wpart_hi = [view(region_g, 8192 * c, F16, 4, D) for c in range(8)]
        wpart_lo = [view(region_g, 8192 * c + 4096, F16, 4, D) for c in range(8)]
        split_rows = view(region_m, 0, F16, FT, 4, 256)
        h_hi, h_lo = split_rows[:, :, 2], split_rows[:, :, 3]
        (hidT_hi, hidT_lo), (xlT_hi, xlT_lo), (xaT_hi, xaT_lo), (yT_hi, yT_lo) = [
            (split_rows[:, K * i:K * i + K, 0], split_rows[:, K * i:K * i + K, 1]) for i in range(4)]
        w_stage = [view(region_x, 8192 * s, F32, 4, D) for s in range(2)]
        hid = view(region_x, 16384, F32, 2, D)
        en = view(region_x, 16384, F32, 2, D)
        xl = view(region_x, 20480, F32, 2, K, P)
        x_res = view(region_x, 20480, F32, 2, D)
        xn = view(region_x, 24576, F32, 2, D)
        h_f = [view(region_x, 28672 + 2048 * i, F32, 2, 256) for i in range(2)]
        y_f = view(region_x, 32768, F32, K, 256)
        y_rows = view(region_x, 32768, F32, 2, D)
        z = view(region_e, 0, F32, 2, D)
        bout_row, battn_row, bnext_row = [view(region_c, b, F32, D) for b in (0, 2048, 5120)]
        fixed = [(view(region_w, 8192 * i, F16, K, D), view(region_w, 8192 * i + 4096, F16, K, D))
                 for i in range(3)]
        (wout_hi, wout_lo), (wattn_hi, wattn_lo), (wnext_hi, wnext_lo) = fixed

        ident = sb("ident", [P, P], F32)
        ident_b = sb("ident_b", [P, P], BF16)
        stats = sb("stats", [P, T, 6], F32)
        mv = sb("mv", [P, T, 2], F32)
        ln_v = sb("ln_v", [P, T], F32)
        minus_half = sb("minus_half", [P, T], F32)
        ln_r = sb("ln_r", [P, T], F32)
        rowsum = sb("rowsum", [P, 2], F32)
        lonely = sb("lonely", [P, 2], F32)
        smax = sb("smax", [P, H], F32)
        smax_all = sb("smax_all", [P, H], F32)
        rden = sb("rden", [P, 2, H], F32)
        b1_col = sb("b1_col", [P, E, FT], F32)
        vec_col = sb("vec_col", [P, VEC], F32)
        b2_col = vec_col[:, 0:E * K].rearrange("p (e k) -> p e k", k=K)
        g_col, b_col = vec_col[:, E * K:E * K + K], vec_col[:, E * K + K:VEC]

        s1T_dram = nc.dram_tensor("s1T_dram", (H, N), F32, kind="Internal").ap()

        ps = ctx.enter_context(nc.psum_tensor("ps", [P, 8, 512], F32))
        ps_adjT = [ps[:, 6 + i, :].bitcast(BF16).rearrange("p (j i) -> p j i", i=P) for i in range(2)]
        ps_tr = [ps[:, u, :].rearrange("p (k c) -> p k c", k=K) for u in range(2)]
        ps_mm = [ps[:, 2 + u, :] for u in range(2)]
        ps_h = [ps[:, 4 + i, :].rearrange("p (f c) -> p f c", f=2) for i in range(2)]
        ps_y = ps[:, 6:8, :].rearrange("p b c -> p (b c)").rearrange("p (k c) -> p k c", k=K)

        ps_wa = ps[:, 4, 0:K * 2 * H].rearrange("p (k i m h) -> p k i m h", k=K, i=2, m=K)

        x_t = x.rearrange("(t p) d -> p t d", p=P)
        x_e = x.rearrange("(u t p) d -> p u t d", p=P, u=2)
        out_e = out.rearrange("(u t p) d -> p u t d", p=P, u=2)
        adj_t = adj.rearrange("(t p) j -> p t j", p=P)
        w1_c = w1.rearrange("e (k p) (c f) -> p e c k f", p=P, c=4)
        w2_c = w2.rearrange("e (c k p) d -> p e c k d", p=P, c=4)

        x_in = [sem(f"x_in{i}") for i in range(4)]
        wseq_in, a_in, wother_in, cols_in = sem("wseq_in"), sem("a_in"), sem("wother_in"), sem("cols_in")
        adj_in = [sem(f"adj_in{u}") for u in range(2)]
        ident_made, cols_turned, cols_evac = sem("ident_made"), sem("cols_turned"), sem("cols_evac")
        wseq_hi_done, wseq_lo_done, wa_step = sem("wseq_hi_done"), sem("wseq_lo_done"), sem("wa_step")
        wT_turned, wT_evac, a_step, wa_made = sem("wT_turned"), sem("wT_evac"), sem("a_step"), sem("wa_made")
        wother_step = sem("wother_step")
        ln_step, ln_root = sem("ln_step"), sem("ln_root")
        xn_ready, xT_done, xhi_done, xlo_done = sem("xn_ready"), sem("xT_done"), sem("xhi_done"), sem("xlo_done")
        s_done, seq_done, s_evac, seq_evac = sem("s_done"), sem("seq_done"), sem("s_evac"), sem("seq_evac")
        adj_cast, lonely_done, adj_bin = sem("adj_cast"), sem("lonely_done"), sem("adj_bin")
        adjT_a, adjT_b, mask_dve, mask_act = sem("adjT_a"), sem("adjT_b"), sem("mask_dve"), sem("mask_act")
        sT_done, sT_evac, s1T_out = sem("sT_done"), sem("sT_evac"), sem("s1T_out")
        smax_done, smax_all_done = sem("smax_done"), sem("smax_all_done")
        coef_step, exp_done = sem("coef_step"), sem("exp_done")
        s1_row_in = [sem(f"s1_row_in{b}") for b in range(2)]
        thr_ready, w_prod_step, w_ready = sem("thr_ready"), sem("w_prod_step"), sem("w_ready")
        act_cmp, dve_cmp, g_ready, g_free = sem("act_cmp"), sem("dve_cmp"), sem("g_ready"), sem("g_free")
        acc_done, lo_copied, acc_free = sem("acc_done"), sem("lo_copied"), sem("acc_free")
        acc_scaled, num_done = sem("acc_scaled"), sem("num_done")
        rows_in = sem("rows_in")
        w_in = [sem(f"w_in{s}") for s in range(2)]
        whi_done, wlo_done = sem("whi_done"), sem("wlo_done")
        rden_done, hid_ready, x_res_in = sem("rden_done"), sem("hid_ready"), sem("x_res_in")
        tr_done, tr_hi, tr_free = sem("tr_done"), sem("tr_hi"), sem("tr_free")
        mo_done, mo_free, ma_done, ma_free = sem("mo_done"), sem("mo_free"), sem("ma_done"), sem("ma_free")
        nx_done, nx_free = sem("nx_done"), sem("nx_free")
        z_ready, en_ready, elu_step = sem("z_ready"), sem("en_ready"), sem("elu_step")
        norm_step, norm_root, xh_ready, xn_done = sem("norm_step"), sem("norm_root"), sem("xh_ready"), sem("xn_done")
        xl_hi_done, xl_lo_done, xa_ready = sem("xl_hi_done"), sem("xl_lo_done"), sem("xa_ready")
        h_done, h_gelu, hhi_done, hlo_done = sem("h_done"), sem("h_gelu"), sem("hhi_done"), sem("hlo_done")
        y_done, y_evac, yhi_done, ylo_done = sem("y_done"), sem("y_evac"), sem("yhi_done"), sem("ylo_done")
        og_ready, out_ready, out_stored = sem("og_ready"), sem("out_ready"), sem("out_stored")

        def settle(eng):
            eng.nop(nofuse=True)

        def splits_in(e, first):
            n = e + 1
            if first:
                return {0: (0, 4), 1: (0, 5), 2: (0, 6), 4: (0, 7), 5: (n, 0), 6: (n, 1), 7: (n, 2)}
            return {1: (n, 0), 3: (n, 1), 5: (n, 2), 7: (n, 3)}

        def wait(eng, semaphore, value):
            if not isinstance(value, int) or value > 0:
                eng.wait_ge(semaphore, value)

        def over_tiles(eng, one, start, stop):
            first, last = LAG + 2, T - 2
            for t in range(start, first):
                one(t, t % 2)
            with eng.Fori(first // 2, last // 2) as i:
                one(2 * i, 0)
                one(2 * i + 1, 1)
            for t in range(last, stop):
                one(t, t % 2)

        def is_tile(t):
            return not isinstance(t, int) or 0 <= t < T

        block = ctx.enter_context(nc.Block())

        @block.sync
        def _(sp):
            sp.dma_start(wseq_f, w_seq.rearrange("(k p) n -> p k n", p=P)).then_inc(wseq_in, 16)
            sp.dma_start(a_row[:, 0, :], a1.partition_broadcast(P)).then_inc(a_in, 16)
            sp.dma_start(a_row[:, 1, :], a2.partition_broadcast(P)).then_inc(a_in, 16)
            for i in range(4):
                sp.dma_start(x_all[:, 4 * i:4 * i + 4, :], x_t[:, 4 * i:4 * i + 4, :]).then_inc(x_in[i], 16)
            for u in range(2):
                sp.dma_start(adj_f[u], adj_t[:, u, :]).then_inc(adj_in[u], 16)
            with sp.Fori(1, T // 2) as i:
                for u in range(2):
                    sp.wait_ge(adj_cast, 2 * i + u - 1)
                    sp.dma_start(adj_f[u], adj_t[:, 2 * i + u, :]).then_inc(adj_in[u], 16)

            def load_s1_row(q, b):
                sp.dma_start(s1_row[b], s1T_dram[bass.ds(2 * q, 2), b * HALF:(b + 1) * HALF]
                             .partition_broadcast(P)).then_inc(s1_row_in[b], 16)

            sp.wait_ge(sT_evac, T)
            sp.dma_start(s1T_dram, s1T[0:H, :]).then_inc(s1T_out, 16)
            sp.wait_ge(s1T_out, 16)
            sp.wait_ge(wother_step, 9)
            for b in range(2):
                load_s1_row(0, b)
            with sp.Fori(1, PAIRS) as q:
                for b in range(2):
                    sp.wait_ge(act_cmp, 16 * q + 8 * b - 8)
                    sp.wait_ge(dve_cmp, 16 * q + 8 * b - 8)
                    load_s1_row(q, b)

            sp.wait_ge(act_cmp, 16 * PAIRS)
            sp.wait_ge(dve_cmp, 16 * PAIRS)

            def load_chunk(e, c, first=False):
                if not first:
                    sp.wait_ge(wlo_done, 8 * e + c - 1)
                src = w1_c[:, e, c] if c < 4 else w2_c[:, e, c - 4]
                sp.dma_start(w_stage[c % 2], src).then_inc(w_in[c % 2], 16)

            for c in range(8):
                load_chunk(0, c, first=(c < 2))
                if c == 1:
                    for row, src in ((bout_row, b_out), (battn_row, attn_b), (bnext_row, next_b)):
                        sp.dma_start(row, src.partition_broadcast(P)).then_inc(rows_in, 16)
                    sp.wait_ge(acc_done, 4 * PAIRS - 4)
                    sp.dma_start(x_res, x_e[:, :, 0, :]).then_inc(x_res_in, 16)
            with sp.Fori(1, E) as e:
                for c in range(8):
                    load_chunk(e, c)
                    if c == 0:
                        sp.wait_ge(xl_lo_done, 2 * e)
                        sp.dma_start(x_res, x_e[:, :, e, :]).then_inc(x_res_in, 16)

        @block.gpsimd
        def _(pool):
            pool.memset(ident[:, :], 0.0).then_inc(ident_made, 1)
            pool.memset(ident_b[:, :], 0.0).then_inc(ident_made, 1)
            pool.wait_ge(ident_made, 2)
            for m in (ident, ident_b):
                pool.affine_select(out=m[:, :], in_=m[:, :], compare_op=ALU.not_equal, fill=1.0, base=0,
                                   pattern=[[-1, P]], channel_multiplier=1).then_inc(ident_made, 1)
            pool.dma_start(b1_rows, b1.rearrange("e (f p) -> (e f) p", p=P)).then_inc(cols_in, 16)
            pool.dma_start(vec_rows[0:E * K], b2.rearrange("e (k p) -> (e k) p", p=P)).then_inc(cols_in, 16)
            pool.dma_start(vec_rows[E * K:E * K + K], ln_g.rearrange("(k p) -> k p", p=P)).then_inc(cols_in, 16)
            pool.dma_start(vec_rows[E * K + K:VEC], ln_b.rearrange("(k p) -> k p", p=P)).then_inc(cols_in, 16)
            pool.memset(minus_half[:, :], -0.5).then_inc(ident_made, 1)
            pool.wait_ge(ident_made, 5)

            def inverse_root(cols, n, root):
                pool.tensor_scalar(ln_v[:, cols], mv[:, cols, 1], EPS, 1.0, ALU.add, ALU.mult).then_inc(root, 1)
                pool.wait_ge(root, n + 1)
                settle(pool)
                pool.tensor_tensor(ln_r[:, cols], ln_v[:, cols], minus_half[:, cols], ALU.pow).then_inc(root, 1)

            for i in range(4):
                pool.wait_ge(ln_step, 2 * i + 2)
                inverse_root(slice(4 * i, 4 * i + 4), 2 * i, ln_root)
            for i, w in enumerate((w_out, attn_w, next_w)):
                hi, lo = fixed[i]
                flat_hi, flat_lo = (a.rearrange("p k n -> p (k n)") for a in (hi, lo))
                if i:
                    pool.wait_ge(wother_step, 3 * i)
                pool.dma_start(wother_f.rearrange("p (k n) -> p k n", k=K),
                               w.rearrange("(k p) n -> p k n", p=P)).then_inc(wother_in, 16)
                pool.wait_ge(wother_in, 16 * (i + 1))
                pool.tensor_scalar(wother_f, wother_f, WS, 1.0, ALU.mult, ALU.mult).then_inc(wother_step, 1)
                pool.wait_ge(wother_step, 3 * i + 1)
                pool.tensor_copy(flat_hi, wother_f).then_inc(wother_step, 1)
                pool.wait_ge(wother_step, 3 * i + 2)
                pool.tensor_tensor(flat_lo, wother_f, flat_hi, ALU.subtract).then_inc(wother_step, 1)
            pool.wait_ge(smax_done, 1)
            pool.partition_all_reduce(smax_all[:, :], smax[:, :], P, bass.bass_isa.ReduceOp.max)\
                .then_inc(smax_all_done, 1)

            def step(e, ffn=True, ahead=True):
                for u in range(2 if ahead else 0):
                    at = 2 * (e + 1) + u
                    pool.wait_ge(norm_step, 2 * at + 2)
                    settle(pool)
                    var, v, r = mv[:, u, 1:2], ln_v[:, 2 * u:2 * u + 2], ln_r[:, 2 * u:2 * u + 2]
                    pool.tensor_scalar(v[:, 0:1], var, EPS, 1.0, ALU.add, ALU.mult).then_inc(norm_root, 1)
                    pool.tensor_scalar(v[:, 1:2], var, 1.0 + EPS, EPS ** 2, ALU.mult, ALU.add).then_inc(norm_root, 1)
                    pool.wait_ge(norm_root, 3 * at + 2)
                    settle(pool)
                    pool.tensor_tensor(r, v, minus_half[:, 0:2], ALU.pow).then_inc(norm_root, 1)
                for u in range(2 if ffn else 0):
                    pool.wait_ge(out_ready, 2 * e + u + 1)
                    pool.dma_start(out_e[:, u, e, :], y_rows[:, u, :]).then_inc(out_stored, 16)

            step(-1, ffn=False)
            step(0)
            with pool.Fori(1, E - 1) as e:
                step(e)
            step(E - 1, ahead=False)
            pool.wait_ge(out_stored, 32 * E)

        @block.tensor
        def _(pe):
            def three(outp, a_hi, a_lo, b_hi, b_lo, start, stop, **kw):
                pe.matmul(outp, a_hi, b_hi, start=start, stop=False, **kw)
                pe.matmul(outp, a_hi, b_lo, start=False, stop=False, **kw)
                return pe.matmul(outp, a_lo, b_hi, start=False, stop=stop, **kw)

            pe.wait_ge(ident_made, 4)
            pe.wait_ge(wseq_in, 16)
            for m in range(K):
                for k in range(K):
                    last = pe.transpose(ps[:, m, k * P:(k + 1) * P], wseq_f[:, k, m * P:(m + 1) * P], ident[:, :])
                last.then_inc(wT_turned, 1)
            pe.wait_ge(a_step, 4)
            pe.wait_ge(wT_evac, K)
            for k in range(K):
                for m in range(K):
                    last = pe.matmul(ps_wa[:, k, :, m, :], wseq_T[:, m, k * P:(k + 1) * P], a_blocks,
                                     start=(k == 0 and m == 0), stop=True, skip_group_check=True)
            last.then_inc(wa_made, 1)

            def turn_columns():
                pe.wait_ge(cols_in, 64)
                pe.transpose(ps[:, 7, 0:P], b1_rows, ident[:, :])
                pe.transpose(ps[:, 7, P:P + VEC], vec_rows[0:VEC], ident[0:VEC, 0:VEC]).then_inc(cols_turned, 1)

            def turn_adjacency(t, u, half):
                read, done = ((mask_dve, adjT_a), (mask_act, adjT_b))[half]
                wait(pe, adj_bin, t + 1)
                if isinstance(t, int) and t == 0:
                    pe.wait_ge(cols_evac, 3)
                wait(pe, read, t)
                for j in range(8):
                    jj = 8 * half + j
                    last = pe.transpose(ps_adjT[half][:, j, :], adj_b[u][:, jj * P:(jj + 1) * P], ident_b[:, :])
                last.then_inc(done, 1)

            def turn_rows(t, u):
                wait(pe, xn_ready, t + 1)
                wait(pe, xlo_done, t - 1)
                for k in range(K):
                    last = pe.transpose(ps[:, u, k * P:(k + 1) * P], xn0[u][:, k * P:(k + 1) * P], ident[:, :])
                last.then_inc(xT_done, 1)

            def scores_and_values(t, u):
                wait(pe, xlo_done, t + 1)
                wait(pe, seq_evac, t - 1)
                wait(pe, sT_evac, t - 1)
                for k in range(K):
                    last = three(ps[:, 4 + u, 0:2 * H], xnT_hi[u][:, k], xnT_lo[u][:, k], wa_hi[:, k], wa_lo[:, k],
                                 k == 0, k == K - 1)
                last.then_inc(s_done, 1)
                for k in range(K):
                    last = three(ps[:, 2 + u, :], xnT_hi[u][:, k], xnT_lo[u][:, k], wseq_hi[:, k], wseq_lo[:, k],
                                 k == 0, k == K - 1)
                last.then_inc(seq_done, 1)

            def turn_s1(t, u):
                wait(pe, s_evac, t + 1)
                pe.transpose(ps[0:H, 4 + u, P:2 * P], s1_now[u], ident[:, :]).then_inc(sT_done, 1)

            def setup(t, u):
                if is_tile(t - 2):
                    turn_s1(t - 2, u)
                if is_tile(t - LAG):
                    turn_adjacency(t - LAG, u, 0)
                if is_tile(t + 1):
                    turn_rows(t + 1, 1 - u)
                if is_tile(t - LAG):
                    turn_adjacency(t - LAG, u, 1)
                if isinstance(t, int) and t == 0:
                    pe.wait_ge(wseq_lo_done, 1)
                    pe.wait_ge(wa_step, 2)
                if isinstance(t, int) and t == LAG - 2:
                    turn_columns()
                if is_tile(t):
                    scores_and_values(t, u)

            over_tiles(pe, setup, -1, T + LAG)

            def chunk(b, w, g, c):
                for j in (2 * c, 2 * c + 1):
                    for a in range(4):
                        acc = ps[:, 4 * g + a, 0:8 * V1]
                        cols = slice((4 * g + a) * P, (4 * g + a + 1) * P)
                        for hh in range(2):
                            last_g = pe.matmul(acc[:, hh * 4 * V1:(hh + 1) * 4 * V1],
                                               g_f8[b][:, j, hh, cols], w[:, j, hh, :],
                                               start=(j == 0 and hh == 0), stop=False,
                                               skip_group_check=True)
                        rows = slice(b * HALF + (4 * g + a) * P, b * HALF + (4 * g + a + 1) * P)
                        last_m = pe.matmul(acc.rearrange("p (x k c) -> p x k c", k=2, c=V1)[:, :, 1, :],
                                           mask_f8[:, j, rows],
                                           w[:, j].rearrange("p h (x k c) -> p (h x) k c", k=2, c=V1)[:, :, 1, :],
                                           start=False, stop=(j == T - 1), skip_group_check=True)
                return last_g, last_m

            def unit(q, b, w, between=None):
                for g in range(2):
                    pe.wait_ge(acc_free, 4 * q + 2 * b + g - 1)
                    for c in range(T // 2):
                        if b == 0 and g == 0 and c == 4:
                            pe.wait_ge(w_ready, 2 * q + 2)
                        if g == 0:
                            pe.wait_ge(g_ready, 16 * q + 8 * b + c + 1)
                        if g == 0 or c == 0:
                            settle(pe)
                        last_g, last_m = chunk(b, w, g, c)
                        if g == 1:
                            last_g.then_inc(g_free, 1)
                            if c == T // 2 - 1:
                                last_m.then_inc(acc_done, 1)
                            if between:
                                between(c)
                    if g == 0:
                        last_m.then_inc(acc_done, 1)

            def first_unit(w):
                for c in range(T // 2):
                    if c == 4:
                        pe.wait_ge(w_ready, 2)
                    pe.wait_ge(g_ready, c + 1)
                    settle(pe)
                    for g in range(2):
                        last_g, last_m = chunk(0, w, g, c)
                        if c == T // 2 - 1:
                            last_m.then_inc(acc_done, 1)
                    last_g.then_inc(g_free, 1)

            pe.wait_ge(mask_act, T)
            pe.wait_ge(mask_dve, T)
            pe.wait_ge(seq_evac, T)
            pe.wait_ge(sT_evac, T)
            pe.wait_ge(w_ready, 1)
            first_unit(w_att[0])
            unit(0, 1, w_att[0])
            with pe.Fori(0, PAIRS // 2 - 1) as i:
                for q, wb in ((2 * i + 1, 1), (2 * i + 2, 0)):
                    pe.wait_ge(w_ready, 2 * q + 1)
                    for b in range(2):
                        unit(q, b, w_att[wb])
            pe.wait_ge(w_ready, 2 * PAIRS - 1)
            unit(PAIRS - 1, 0, w_att[1])

            def transpose_rows(src, stage, n, u, ready):
                pe.wait_ge(ready, 2 * n + u + 1)
                if not (isinstance(n, int) and n == 0 and stage == 0):
                    pe.wait_ge(tr_free, 6 * n + 2 * stage + u - 1)
                for k in range(K):
                    last = pe.transpose(ps_tr[u][:, k, :], src[:, u, k * P:(k + 1) * P], ident[:, :])
                last.then_inc(tr_done, 1)

            def project(a_hi, a_lo, b_hi, b_lo, u, done):
                rows = slice(u * P, (u + 1) * P)
                for k in range(K):
                    last = three(ps_mm[u], a_hi[:, k, rows], a_lo[:, k, rows], b_hi[:, k], b_lo[:, k],
                                 k == 0, k == K - 1)
                last.then_inc(done, 1)

            def out_projection(n, u, e=None):
                pe.wait_ge(tr_free, 6 * n + u + 1)
                if e is not None:
                    pe.wait_ge(nx_free, 2 * e)
                project(hidT_hi, hidT_lo, wout_hi, wout_lo, u, mo_done)

            def dense(n, u):
                pe.wait_ge(xl_lo_done, 2 * n + u + 1)
                pe.wait_ge(mo_free, 2 * n + u + 1)
                project(xlT_hi, xlT_lo, wattn_hi, wattn_lo, u, ma_done)

            def w1_tiles(e, fp, first=False):
                c = fp // 2
                if fp % 2 == 0:
                    pe.wait_ge(wlo_done, 8 * e + c + 1)
                if fp == 0:
                    pe.wait_ge(tr_free, 6 * e + 6)
                if not (first and fp < 2):
                    pe.wait_ge(h_gelu, 8 * e + fp - 1)
                for f in range(2):
                    cols = slice((2 * fp + f) % 4 * P, ((2 * fp + f) % 4 + 1) * P)
                    for k in range(K):
                        last = three(ps_h[fp % 2][:, f, :], wpart_hi[c][:, k, cols], wpart_lo[c][:, k, cols],
                                     xaT_hi[:, k], xaT_lo[:, k], k == 0, k == K - 1)
                last.then_inc(h_done, 1)

            def w2_tiles(e, c, ds, first):
                if ds[0] == 0:
                    pe.wait_ge(wlo_done, 8 * e + c + 5)
                    pe.wait_ge(hlo_done, 8 * e + 2 * c + 2)
                    if c == 0 and not first:
                        pe.wait_ge(y_evac, 2 * e)
                for f in range(4):
                    ft = 4 * c + f
                    for d in ds:
                        last = three(ps_y[:, d, :], wpart_hi[4 + c][:, f, d * P:(d + 1) * P],
                                     wpart_lo[4 + c][:, f, d * P:(d + 1) * P], h_hi[:, ft], h_lo[:, ft],
                                     ft == 0 and d % 2 == 0, ft == FT - 1, skip_group_check=True)
                last.then_inc(y_done, 1)

            def next_rows(e):
                for kk in range(2):
                    pe.wait_ge(ylo_done, 2 * e + kk + 1)
                    for u in range(2):
                        for k in (2 * kk, 2 * kk + 1):
                            rows = slice(u * P, (u + 1) * P)
                            last = three(ps_mm[u], yT_hi[:, k, rows], yT_lo[:, k, rows], wnext_hi[:, k],
                                         wnext_lo[:, k], k == 0, k == K - 1)
                        if kk == 1:
                            last.then_inc(nx_done, 1)

            def between(c):
                if c == 0:
                    pe.wait_ge(wother_step, 9)
                    pe.wait_ge(acc_free, 4 * PAIRS - 1)
                    transpose_rows(hid, 0, 0, 0, hid_ready)
                elif c == 2:
                    transpose_rows(hid, 0, 0, 1, hid_ready)
                    out_projection(0, 0)
                elif c == 3:
                    out_projection(0, 1)
                elif c == 6:
                    transpose_rows(z, 1, 0, 0, xh_ready)

            def step(e, ahead=True, first=False):
                n = e + 1
                w1_tiles(e, 0, first)
                w1_tiles(e, 1, first)
                if ahead:
                    for u in range(2):
                        transpose_rows(hid, 0, n, u, hid_ready)
                w1_tiles(e, 2)
                w1_tiles(e, 3)
                if ahead:
                    for u in range(2):
                        out_projection(n, u, None if first else e)
                for fp in range(4, 8):
                    w1_tiles(e, fp)
                w2_tiles(e, 0, range(4), first)
                if ahead:
                    for u in range(2):
                        transpose_rows(z, 1, n, u, xh_ready)
                w2_tiles(e, 1, range(4), first)
                w2_tiles(e, 2, range(4), first)
                if ahead:
                    for u in range(2):
                        dense(n, u)
                w2_tiles(e, 3, range(0, 2), first)
                w2_tiles(e, 3, range(2, 4), first)
                if ahead:
                    for u in range(2):
                        transpose_rows(z, 2, n, u, xa_ready)
                    pe.wait_ge(ma_free, 2 * n + 2)
                else:
                    pe.wait_ge(nx_free, 2 * e)
                next_rows(e)

            unit(PAIRS - 1, 1, w_att[1], between)
            transpose_rows(z, 1, 0, 1, xh_ready)
            for u in range(2):
                dense(0, u)
            for u in range(2):
                transpose_rows(z, 2, 0, u, xa_ready)
            pe.wait_ge(acc_free, 4 * PAIRS)
            step(0, first=True)
            with pe.Fori(1, E - 1) as e:
                step(e)
            step(E - 1, ahead=False)

        @block.scalar
        def _(act):
            act.wait_ge(wseq_in, 16)
            act.activation(wseq_hi, wseq_f, ACT.Copy, scale=WS).then_inc(wseq_hi_done, 1)
            for m in range(K):
                act.wait_ge(wT_turned, m + 1)
                act.activation(wseq_T[:, m, :], ps[:, m, :], ACT.Copy).then_inc(wT_evac, 1)

            def cast(t, u):
                wait(act, adj_in[u], 16 * (t // 2 + 1) if isinstance(t, int) else 8 * (t - u) + 16)
                wait(act, adjT_b, t - 1)
                act.activation(adj_b[u], adj_f[u], ACT.Copy, accum_out=rowsum[:, u:u + 1]).then_inc(adj_cast, 1)

            def high_rows(t, u):
                wait(act, xT_done, t + 1)
                wait(act, seq_done, t - 1)
                act.activation(xnT_hi[u].rearrange("p k c -> p (k c)"), ps[:, u, :], ACT.Copy, scale=XS)\
                    .then_inc(xhi_done, 1)

            def setup(t, u):
                if is_tile(t - 2):
                    wait(act, sT_done, t - 1)
                    act.activation(s1T[0:H, bass.ds((t - 2) * P, P)], ps[0:H, 4 + u, P:2 * P], ACT.Copy)\
                        .then_inc(sT_evac, 1)
                if is_tile(t + 1):
                    high_rows(t + 1, 1 - u)
                if is_tile(t - LAG + 2):
                    cast(t - LAG + 2, u)
                if is_tile(t - LAG):
                    wait(act, adjT_b, t - LAG + 1)
                    act.activation(mask_u8[:, 8:16, bass.ds((t - LAG) * P, P)], ps_adjT[1], ACT.Copy, scale=NEG1)\
                        .then_inc(mask_act, 1)

            over_tiles(act, setup, -2, T + 2)
            act.wait_ge(coef_step, 3)
            act.activation(e_b, su, ACT.Exp).then_inc(exp_done, 1)
            act.activation(e_d, su, ACT.Exp, scale=0.2).then_inc(exp_done, 1)
            setup(T + 2, 0)
            act.wait_ge(coef_step, 5)
            act.activation(c_row, st_c, ACT.Exp).then_inc(exp_done, 1)
            setup(T + 3, 1)

            def copy_low(q, b, g):
                group = 4 * q + 2 * b + g
                act.wait_ge(acc_done, group + 1)
                act.activation(acc_lo[g], ps[:, 4 * g:4 * g + 4, 0:8 * V1]
                               .rearrange("p a (h x c) -> p a h x c", h=2, x=2)[:, :, :, 1, :], ACT.Copy)\
                    .then_inc(lo_copied, 1)

            def compare_unit(q, b, tb, copies, free):
                act.wait_ge(s1_row_in[b], 16 * (q + 1))
                for c in range(T // 2):
                    if c in copies:
                        copy_low(*copies[c])
                    if free:
                        act.wait_ge(g_free, 16 * (q - 1) + 8 * b + c + 1)
                    if free or c == 0:
                        settle(act)
                    for j in (2 * c, 2 * c + 1):
                        for hh in range(2):
                            if (b, j, hh) not in DVE_CMP:
                                last = act.activation(g_f8[b][:, j, hh, :], s1_row[b][:, hh, :], ACT.Sigmoid,
                                                      bias=thr_now[tb][:, 1, j, hh:hh + 1], scale=BIG,
                                                      saturate=False)
                    last.then_inc(act_cmp, 1)

            def copies_in(q, b):
                return {0: (q - 1, b, 1), 4: (q, 0, 0) if b else (q - 1, 1, 0)}

            def pair(q, tb):
                act.wait_ge(thr_ready, q + 1)
                for b in range(2):
                    compare_unit(q, b, tb, copies_in(q, b), True)

            act.wait_ge(adjT_b, T)
            act.wait_ge(thr_ready, 1)
            compare_unit(0, 0, 0, {}, False)
            compare_unit(0, 1, 0, {2: (0, 0, 0), 3: (0, 0, 1)}, False)
            act.wait_ge(thr_ready, 2)
            compare_unit(1, 0, 1, {4: (0, 1, 0)}, True)
            compare_unit(1, 1, 1, copies_in(1, 1), True)
            with act.Fori(1, PAIRS // 2 - 1) as i:
                pair(2 * i, 0)
                pair(2 * i + 1, 1)
            pair(PAIRS - 2, 0)
            pair(PAIRS - 1, 1)

            def split_chunk(e, c):
                act.wait_ge(w_in[c % 2], 16 * (4 * e + c // 2 + 1))
                if isinstance(e, int) and e == 0:
                    act.wait_ge(acc_done, 4 * PAIRS - 2 if c < 4 else 4 * PAIRS)
                elif c < 4:
                    act.wait_ge(h_done, 8 * (e - 1) + 2 * c + 2)
                else:
                    act.wait_ge(y_done, 5 * (e - 1) + (c - 3 if c < 7 else 5))
                act.activation(wpart_hi[c], w_stage[c % 2], ACT.Copy, scale=WS).then_inc(whi_done, 1)

            def transposed_hi(dst, stage, n, u):
                act.wait_ge(tr_done, 6 * n + 2 * stage + u + 1)
                act.activation(dst[:, :, u * P:(u + 1) * P], ps_tr[u], ACT.Copy, scale=XS).then_inc(tr_hi, 1)

            def elu_exp(n, u):
                act.wait_ge(z_ready, 2 * n + u + 1)
                act.activation(en[:, u, :], z[:, u, :], ACT.Exp).then_inc(en_ready, 1)

            def gain_hi(n, u):
                act.wait_ge(tr_free, 6 * n + 2 + u + 1)
                act.activation(xlT_hi[:, :, u * P:(u + 1) * P], xl[:, u], ACT.Copy, scale=XS).then_inc(xl_hi_done, 1)

            def gelu(e, fp, first=False):
                act.wait_ge(h_done, 8 * e + fp + 1)
                if not (first and fp < 2):
                    act.wait_ge(hlo_done, 8 * e + fp - 1)
                for f in range(2):
                    bias = b1_col[:, bass.ds(e, 1), 2 * fp + f:2 * fp + f + 1].rearrange("p a b -> p (a b)")
                    last = act.activation(h_f[fp % 2][:, f, :], ps_h[fp % 2][:, f, :], ACT.Gelu,
                                          bias=bias, scale=1.0 / (WS * XS))
                last.then_inc(h_gelu, 1)

            def step(e, ahead=True, first=False):
                n = e + 1
                splits = splits_in(e, first) if ahead else {}
                for fp in range(8):
                    gelu(e, fp, first)
                    if fp == 1 and ahead:
                        for u in range(2):
                            transposed_hi(hidT_hi, 0, n, u)
                    if fp == 4 and ahead:
                        for u in range(2):
                            elu_exp(n, u)
                    if fp in splits:
                        split_chunk(*splits[fp])
                if ahead:
                    for u in range(2):
                        gain_hi(n, u)
                    for c in (3, 4) if first else (4, 5, 6):
                        split_chunk(n, c)
                    for u in range(2):
                        transposed_hi(xaT_hi, 2, n, u)
                    for c in (5, 6, 7) if first else (7,):
                        split_chunk(n, c)
                for u in range(2):
                    act.wait_ge(nx_free, 2 * e + u + 1)
                    act.activation(y_rows[:, u, :], y_rows[:, u, :], ACT.Gelu).then_inc(og_ready, 1)

            act.wait_ge(cols_evac, 3)
            copy_low(PAIRS - 1, 0, 1)
            split_chunk(0, 0)
            copy_low(PAIRS - 1, 1, 0)
            for u in range(2):
                transposed_hi(hidT_hi, 0, 0, u)
            split_chunk(0, 1)
            for u in range(2):
                elu_exp(0, u)
            split_chunk(0, 2)
            gain_hi(0, 0)
            copy_low(PAIRS - 1, 1, 1)
            gain_hi(0, 1)
            split_chunk(0, 3)
            for u in range(2):
                transposed_hi(xaT_hi, 2, 0, u)
            step(0, first=True)
            with act.Fori(1, E - 1) as e:
                step(e)
            step(E - 1, ahead=False)

        @block.vector
        def _(dve):
            dve.wait_ge(a_in, 32)
            dve.wait_ge(ident_made, 4)
            for i in range(2):
                if i:
                    dve.wait_ge(a_step, 2)
                dve.tensor_tensor(a_prod, ident[:, :].rearrange("p (h c) -> p h c", c=DH),
                                  a_row[:, i:i + 1, :].to_broadcast([P, P // DH, DH]), ALU.mult).then_inc(a_step, 1)
                dve.wait_ge(a_step, 2 * i + 1)
                dve.tensor_reduce(a_blocks[:, i, :], a_prod, AX.X, ALU.add).then_inc(a_step, 1)
            dve.wait_ge(wseq_hi_done, 1)
            dve.scalar_tensor_tensor(wseq_lo, wseq_f, WS, wseq_hi, ALU.mult, ALU.subtract).then_inc(wseq_lo_done, 1)

            def row_statistics(i):
                dve.wait_ge(x_in[i], 16)
                for t in range(4 * i, 4 * i + 4):
                    last = dve.bn_stats(stats[:, t, :], x_all[:, t, :])
                last.then_inc(ln_step, 1)
                dve.wait_ge(ln_step, 2 * i + 1)
                for t in range(4 * i, 4 * i + 4):
                    last = dve.bn_aggr(mv[:, t, :], stats[:, t, :])
                last.then_inc(ln_step, 1)

            row_statistics(0)
            wah_flat, wal_flat = wa_hi.rearrange("p k c -> p (k c)"), wa_lo.rearrange("p k c -> p (k c)")
            dve.wait_ge(wa_made, 1)
            dve.tensor_scalar(wah_flat, ps[:, 4, 0:K * 2 * H], WS, None, ALU.mult).then_inc(wa_step, 1)
            dve.wait_ge(wa_step, 1)
            dve.scalar_tensor_tensor(wal_flat, ps[:, 4, 0:K * 2 * H], WS, wah_flat, ALU.mult, ALU.subtract)\
                .then_inc(wa_step, 1)
            dve.memset(seqv[:, :, DH::V1], 1.0)
            def take_columns():
                dve.wait_ge(cols_turned, 1)
                dve.tensor_copy(b1_col[:, :, :].rearrange("p e f -> p (e f)"), ps[:, 7, 0:P]).then_inc(cols_evac, 1)
                dve.tensor_scalar(vec_col[:, 0:E * K], ps[:, 7, P:P + E * K], HS, None, ALU.mult).then_inc(cols_evac, 1)
                dve.tensor_copy(vec_col[:, E * K:VEC], ps[:, 7, P + E * K:P + VEC]).then_inc(cols_evac, 1)

            def normal_rows(t, u):
                if isinstance(t, int) and t in (0, 4):
                    dve.wait_ge(ln_root, 2 if t == 0 else 8)
                wait(dve, xT_done, t - 1)
                mean = mv[:, bass.ds(t, 1), 0:1].rearrange("p a b -> p (a b)")
                dve.tensor_scalar(xn0[u], x_all[:, bass.ds(t, 1), :].rearrange("p t d -> p (t d)"), mean,
                                  ln_r[:, bass.ds(t, 1)], ALU.subtract, ALU.mult).then_inc(xn_ready, 1)

            def setup(t, u):
                if is_tile(t + 2):
                    normal_rows(t + 2, u)
                if isinstance(t, int) and t in (-1, 0, 1):
                    row_statistics(t + 2)
                if isinstance(t, int) and t == LAG - 1:
                    take_columns()
                a = t - LAG
                if is_tile(a + 1):
                    wait(dve, adj_cast, a + 2)
                    dve.tensor_scalar(lonely[:, 1 - u:2 - u], rowsum[:, 1 - u:2 - u], 0.5, None, ALU.is_lt)\
                        .then_inc(lonely_done, 1)
                if is_tile(a):
                    wait(dve, adjT_a, a + 1)
                    dve.tensor_scalar(mask_u8[:, 0:8, bass.ds(a * P, P)], ps_adjT[0], NEG1, None, ALU.mult)\
                        .then_inc(mask_dve, 1)
                if is_tile(a + 1):
                    wait(dve, lonely_done, a + 2)
                    dve.tensor_scalar(adj_b[1 - u], adj_b[1 - u], lonely[:, 1 - u:2 - u], None, ALU.max)\
                        .then_inc(adj_bin, 1)
                if is_tile(t + 1):
                    wait(dve, xhi_done, t + 2)
                    wait(dve, seq_done, t)
                    dve.scalar_tensor_tensor(xnT_lo[1 - u].rearrange("p k c -> p (k c)"), ps[:, 1 - u, :], XS,
                                             xnT_hi[1 - u].rearrange("p k c -> p (k c)"), ALU.mult, ALU.subtract)\
                        .then_inc(xlo_done, 1)
                if is_tile(t - 1):
                    wait(dve, s_done, t)
                    wait(dve, sT_done, t - 2)
                    dve.tensor_scalar(s1_now[1 - u], ps[:, 5 - u, 0:H], 1.0 / (WS * XS), None, ALU.mult)
                    dve.tensor_scalar(s12[:, bass.ds(t - 1, 1), :].rearrange("p t h -> p (t h)"),
                                      ps[:, 5 - u, 0:2 * H], 1.0 / (WS * XS), None, ALU.mult).then_inc(s_evac, 1)
                    wait(dve, seq_done, t)
                    dve.tensor_scalar(seqv[:, bass.ds(t - 1, 1), :].rearrange("p t (h c) -> p (t h) c", c=V1)[:, :, 0:DH],
                                      ps[:, 3 - u, :].rearrange("p (h c) -> p h c", c=DH),
                                      1.0 / (WS * XS), None, ALU.mult).then_inc(seq_evac, 1)

            over_tiles(dve, setup, -2, T + 1)

            def take_thr(q, wb):
                dve.tensor_copy(thr_now[wb][:, :, :, :].rearrange("p k t h -> p (k t h)"),
                                thr[:, bass.ds(q, 1)].rearrange("p q k t h -> p (q k t h)")).then_inc(thr_ready, 1)

            def make_w(q, wb, jb, first=False):
                js = slice(8 * jb, 8 * jb + 8)
                if not first:
                    dve.wait_ge(w_ready, 2 * q + jb)
                v = seqv[:, js, bass.ds(2 * q * V1, 2 * V1)].rearrange("p t (h c) -> p t h c", c=V1)
                for kind, coef in ((0, e_b), (1, e_d)):
                    f = coef[:, js, bass.ds(2 * q, 2)].unsqueeze(3).to_broadcast([P, 8, 2, V1])
                    dve.tensor_tensor(w_prod[:, :, :, kind * V1:(kind + 1) * V1], v, f, ALU.mult)\
                        .then_inc(w_prod_step, 1)
                dve.wait_ge(w_prod_step, 6 * q + 3 * jb + 2)
                hi, lo = w_att[wb][:, js, :, 0:2 * V1], w_att[wb][:, js, :, 2 * V1:4 * V1]
                dve.tensor_copy(hi, w_prod).then_inc(w_prod_step, 1)
                dve.wait_ge(w_prod_step, 6 * q + 3 * jb + 3)
                dve.tensor_tensor(lo, w_prod, hi, ALU.subtract).then_inc(w_ready, 1)

            dve.wait_ge(s_evac, T)
            s1, s2 = s12[:, :, 0:H], s12[:, :, H:2 * H]
            dve.tensor_reduce(smax[:, :], s2.rearrange("p t h -> p h t"), AX.X, ALU.max).then_inc(smax_done, 1)
            by_pair = s2.rearrange("p t (q h) -> p t q h", h=2)
            for kind, factor in ((0, -1.0), (1, BIG)):
                dve.tensor_scalar(thr[:, :, kind].rearrange("p q t h -> p t q h"), by_pair, factor, None, ALU.mult)\
                    .then_inc(coef_step, 1)
            setup(T + 1, 1)
            dve.wait_ge(smax_all_done, 1)
            top = smax_all[:, :].unsqueeze(1).to_broadcast([P, T, H])
            dve.tensor_tensor(su, s2, top, ALU.subtract).then_inc(coef_step, 1)
            dve.tensor_tensor(st_c, s1, top, ALU.add).then_inc(coef_step, 1)
            dve.wait_ge(coef_step, 4)
            dve.tensor_scalar(st_c, st_c, -0.8, 0.0, ALU.mult, ALU.min).then_inc(coef_step, 1)
            setup(T + 2, 0)
            dve.wait_ge(exp_done, 2)
            dve.tensor_scalar(e_b, e_b, KAPPA, None, ALU.mult).then_inc(coef_step, 1)
            dve.tensor_scalar(e_d, e_d, -KAPPA, None, ALU.mult).then_inc(coef_step, 1)
            dve.wait_ge(seq_evac, T)
            dve.wait_ge(coef_step, 7)
            take_thr(0, 0)
            make_w(0, 0, 0, first=True)
            setup(T + 3, 1)

            def acc_add(q, b, g):
                group = 4 * q + 2 * b + g
                dve.wait_ge(lo_copied, group + 1)
                dve.tensor_tensor(acc_s[g], ps[:, 4 * g:4 * g + 4, 0:8 * V1]
                                  .rearrange("p a (h x c) -> p a h x c", h=2, x=2)[:, :, :, 0, :],
                                  acc_lo[g], ALU.add).then_inc(acc_free, 1)

            def acc_scale(q, b, g):
                group = 4 * q + 2 * b + g
                dve.wait_ge(acc_free, group + 1)
                s = acc_s[g][:, :, :, V1:2 * V1]
                t0 = 8 * b + 4 * g
                coef = c_row[:, t0:t0 + 4, bass.ds(2 * q, 2)]
                dve.tensor_tensor(s, s, coef.unsqueeze(3).to_broadcast([P, 4, 2, V1]), ALU.mult)\
                    .then_inc(acc_scaled, 1)

            def acc_sum(q, b, g):
                group = 4 * q + 2 * b + g
                dve.wait_ge(acc_scaled, group + 1)
                t0 = 8 * b + 4 * g
                dst = seqv[:, t0:t0 + 4, bass.ds(2 * q * V1, 2 * V1)].rearrange("p t (h c) -> p t h c", c=V1)
                dve.tensor_tensor(dst, acc_s[g][:, :, :, 0:V1], acc_s[g][:, :, :, V1:2 * V1], ALU.add)\
                    .then_inc(num_done, 1)

            def mask_chunk(q, b, c):
                dve.wait_ge(act_cmp, 16 * q + 8 * b + c + 1)
                dve.wait_ge(dve_cmp, 16 * q + 8 * b + c + 1)
                g = g_u32[b][:, 2 * c:2 * c + 2]
                m = mask_u32[:, 2 * c:2 * c + 2, b * HALF // 4:(b + 1) * HALF // 4]
                dve.tensor_tensor(g, g, m.unsqueeze(2).to_broadcast([P, 2, 2, HALF // 4]), ALU.bitwise_and)\
                    .then_inc(g_ready, 1)

            def sums_in(q, b):
                groups = ((0, (q - 1, b, 1)), (4, (q, 0, 0) if b else (q - 1, 1, 0)))
                return {c: (f, group) for c0, group in groups
                        for c, f in zip(range(c0, c0 + 3), (acc_add, acc_scale, acc_sum))}

            def unit(q, b, tb, sums, free=True, next_pair=True):
                dve.wait_ge(s1_row_in[b], 16 * (q + 1))
                for c in range(T // 2):
                    if c in sums:
                        f, group = sums[c]
                        f(*group)
                    if b == 0 and c == 2:
                        if free:
                            wait(dve, g_free, 16 * (q - 1))
                        make_w(q, tb, 1)
                    if b == 1 and c == 5 and next_pair:
                        if free:
                            dve.wait_ge(g_free, 16 * (q - 1) + 12)
                        take_thr(q + 1, 1 - tb)
                        make_w(q + 1, 1 - tb, 0)
                    if free:
                        dve.wait_ge(g_free, 16 * (q - 1) + 8 * b + c + 1)
                    for j in (2 * c, 2 * c + 1):
                        for hh in range(2):
                            if (b, j, hh) in DVE_CMP:
                                last = dve.tensor_scalar(g_u8[b][:, j, hh, :], s1_row[b][:, hh, :],
                                                         thr_now[tb][:, 0, j, hh:hh + 1], POS1, ALU.is_gt, ALU.mult)
                    last.then_inc(dve_cmp, 1)
                    if c:
                        mask_chunk(q, b, c - 1)
                mask_chunk(q, b, T // 2 - 1)

            def pair(q, tb, **kw):
                for b in range(2):
                    unit(q, b, tb, sums_in(q, b), **kw)

            dve.wait_ge(mask_act, T)
            dve.wait_ge(mask_dve, T)
            dve.wait_ge(exp_done, 3)
            unit(0, 0, 0, {}, free=False)
            first = [(f, (0, 0, g)) for f in (acc_add, acc_scale, acc_sum) for g in range(2)]
            unit(0, 1, 0, dict(zip(range(2, 8), first)), free=False)
            unit(1, 0, 1, {c: of for c, of in sums_in(1, 0).items() if c >= 4})
            unit(1, 1, 1, sums_in(1, 1))
            with dve.Fori(1, PAIRS // 2 - 1) as i:
                pair(2 * i, 0)
                pair(2 * i + 1, 1)
            pair(PAIRS - 2, 0)
            pair(PAIRS - 1, 1, next_pair=False)

            rows = seqv.rearrange("p (u t) c -> p u t c", u=2)

            def tile_of(e, u, n=H * V1):
                return rows[:, u:u + 1, bass.ds(e, 1), 0:n].rearrange("p u t c -> p (u t c)")

            def split_chunk(n, c):
                dve.wait_ge(whi_done, 8 * n + c + 1)
                dve.scalar_tensor_tensor(wpart_lo[c], w_stage[c % 2], WS, wpart_hi[c], ALU.mult, ALU.subtract)\
                    .then_inc(wlo_done, 1)

            def transposed_lo(dst, hi, stage, n, u):
                part = slice(u * P, (u + 1) * P)
                dve.wait_ge(tr_hi, 4 * n + stage + u + 1)
                dve.scalar_tensor_tensor(dst[:, :, part], ps_tr[u], XS, hi[:, :, part],
                                         ALU.mult, ALU.subtract).then_inc(tr_free, 1)

            def hidden(e, u):
                num = tile_of(e, u).rearrange("p (h c) -> p h c", c=V1)
                dve.reciprocal(rden[:, u, :], num[:, :, DH]).then_inc(rden_done, 1)
                dve.wait_ge(rden_done, 2 * e + u + 1)
                dve.tensor_tensor(hid[:, u, :].rearrange("p (h c) -> p h c", c=DH), num[:, :, 0:DH],
                                  rden[:, u, :].unsqueeze(2).to_broadcast([P, H, DH]), ALU.mult)\
                    .then_inc(hid_ready, 1)

            def elu_in(e, u):
                dve.wait_ge(mo_done, 2 * e + u + 1)
                dve.scalar_tensor_tensor(z[:, u, :], ps_mm[u], 1.0 / (WS * XS), bout_row, ALU.mult, ALU.add)\
                    .then_inc(mo_free, 1)
                dve.wait_ge(mo_free, 2 * e + u + 1)
                dve.tensor_scalar(xn[:, u, :], z[:, u, :], 0.0, None, ALU.max).then_inc(z_ready, 1)

            def elu_out(e, u):
                dve.wait_ge(en_ready, 2 * e + u + 1)
                dve.scalar_tensor_tensor(z[:, u, :], en[:, u, :], 1.0, xn[:, u, :], ALU.min, ALU.add)\
                    .then_inc(elu_step, 1)
                dve.wait_ge(elu_step, 4 * e + 2 * u + 1)
                dve.wait_ge(x_res_in, 16 * (e + 1))
                x1 = tile_of(e, u, D)
                dve.scalar_tensor_tensor(x1, z[:, u, :], -1.0, x_res[:, u, :], ALU.add, ALU.add).then_inc(elu_step, 1)
                dve.wait_ge(elu_step, 4 * e + 2 * u + 2)
                settle(dve)
                dve.bn_stats(stats[:, u, :], x1).then_inc(norm_step, 1)
                dve.wait_ge(norm_step, 4 * e + 2 * u + 1)
                settle(dve)
                dve.bn_aggr(mv[:, u, :], stats[:, u, :]).then_inc(norm_step, 1)

            def norms(e, u):
                dve.wait_ge(norm_root, 3 * (2 * e + u) + 3)
                for dst, root, done in ((z, 1, xh_ready), (xn, 0, xn_done)):
                    dve.tensor_scalar(dst[:, u, :], tile_of(e, u, D), mv[:, u, 0:1],
                                      ln_r[:, 2 * u + root:2 * u + root + 1], ALU.subtract, ALU.mult).then_inc(done, 1)

            def gain(e, u):
                dve.wait_ge(tr_done, 6 * e + 2 + u + 1)
                for k in range(K):
                    last = dve.tensor_scalar(xl[:, u, k, :], ps_tr[u][:, k, :], g_col[:, k:k + 1], b_col[:, k:k + 1],
                                             ALU.mult, ALU.add)
                last.then_inc(tr_free, 1)

            def gain_lo(e, u):
                part = slice(u * P, (u + 1) * P)
                dve.wait_ge(xl_hi_done, 2 * e + u + 1)
                dve.scalar_tensor_tensor(xlT_lo[:, :, part], xl[:, u], XS, xlT_hi[:, :, part], ALU.mult, ALU.subtract)\
                    .then_inc(xl_lo_done, 1)

            def dense_out(e, u):
                dve.wait_ge(ma_done, 2 * e + u + 1)
                dve.scalar_tensor_tensor(z[:, u, :], ps_mm[u], 1.0 / (WS * XS), battn_row, ALU.mult, ALU.add)\
                    .then_inc(ma_free, 1)
                dve.wait_ge(ma_free, 2 * e + u + 1)
                dve.wait_ge(xn_done, 2 * e + u + 1)
                dve.tensor_tensor(z[:, u, :], z[:, u, :], xn[:, u, :], ALU.add).then_inc(xa_ready, 1)

            def split_h(e, fp, first):
                dve.wait_ge(h_gelu, 8 * e + fp + 1)
                if not first:
                    dve.wait_ge(y_done, 5 * e)
                pair_of = slice(2 * fp, 2 * fp + 2)
                dve.tensor_scalar(h_hi[:, pair_of], h_f[fp % 2], HS, None, ALU.mult).then_inc(hhi_done, 1)
                dve.wait_ge(hhi_done, 8 * e + fp + 1)
                dve.scalar_tensor_tensor(h_lo[:, pair_of], h_f[fp % 2], HS, h_hi[:, pair_of],
                                         ALU.mult, ALU.subtract).then_inc(hlo_done, 1)

            def y_out(e, kk, first):
                dve.wait_ge(y_done, 5 * e + 4 + kk)
                if not kk and not first:
                    dve.wait_ge(out_stored, 32 * e)
                ks = slice(2 * kk, 2 * kk + 2)
                for k in (2 * kk, 2 * kk + 1):
                    bias = b2_col[:, bass.ds(e, 1), k:k + 1].rearrange("p a b -> p (a b)")
                    last = dve.tensor_scalar(y_f[:, k, :], ps_y[:, k, :], 1.0 / WS, bias, ALU.mult, ALU.add)
                last.then_inc(y_evac, 1)
                dve.wait_ge(y_evac, 2 * e + kk + 1)
                dve.tensor_copy(yT_hi[:, ks], y_f[:, ks]).then_inc(yhi_done, 1)
                dve.wait_ge(yhi_done, 2 * e + kk + 1)
                dve.tensor_tensor(yT_lo[:, ks], y_f[:, ks], yT_hi[:, ks], ALU.subtract).then_inc(ylo_done, 1)

            def next_out(e, u):
                dve.wait_ge(nx_done, 2 * e + u + 1)
                dve.scalar_tensor_tensor(y_rows[:, u, :], ps_mm[u], 1.0 / (WS * HS), bnext_row, ALU.mult, ALU.add)\
                    .then_inc(nx_free, 1)

            def residual_out(e, u):
                dve.wait_ge(og_ready, 2 * e + u + 1)
                dve.tensor_tensor(y_rows[:, u, :], y_rows[:, u, :], tile_of(e, u, D), ALU.add).then_inc(out_ready, 1)

            def step(e, ahead=True, first=False):
                n = e + 1

                def both(stage, *args):
                    for u in range(2):
                        stage(*args, n, u)

                splits = splits_in(e, first) if ahead else {}
                if ahead:
                    both(hidden)
                for fp in range(8):
                    split_h(e, fp, first)
                    if fp == 0 and not first:
                        split_chunk(e, 7)
                    if ahead:
                        if fp == 1:
                            both(transposed_lo, hidT_lo, hidT_hi, 0)
                        if fp in splits:
                            split_chunk(*splits[fp])
                        if fp == 3:
                            both(elu_in)
                        if fp == 4:
                            both(elu_out)
                        if fp == 5:
                            both(norms)
                if ahead:
                    both(gain)
                    both(gain_lo)
                    for c in (3, 4) if first else (4, 5):
                        split_chunk(n, c)
                    both(dense_out)
                y_out(e, 0, first)
                y_out(e, 1, first)
                if ahead:
                    both(transposed_lo, xaT_lo, xaT_hi, 2)
                    for c in (5, 6) if first else (6,):
                        split_chunk(n, c)
                for u in range(2):
                    next_out(e, u)
                for u in range(2):
                    residual_out(e, u)

            def last_sum(b, g):
                acc_add(PAIRS - 1, b, g)
                acc_scale(PAIRS - 1, b, g)
                acc_sum(PAIRS - 1, b, g)

            dve.wait_ge(num_done, 4 * PAIRS - 3)
            hidden(0, 0)
            last_sum(0, 1)
            last_sum(1, 0)
            dve.wait_ge(num_done, 4 * PAIRS - 1)
            hidden(0, 1)
            transposed_lo(hidT_lo, hidT_hi, 0, 0, 0)
            split_chunk(0, 0)
            transposed_lo(hidT_lo, hidT_hi, 0, 0, 1)
            split_chunk(0, 1)
            dve.wait_ge(rows_in, 48)
            elu_in(0, 0)
            elu_out(0, 0)
            elu_in(0, 1)
            norms(0, 0)
            elu_out(0, 1)
            gain(0, 0)
            gain_lo(0, 0)
            norms(0, 1)
            gain(0, 1)
            gain_lo(0, 1)
            dense_out(0, 0)
            last_sum(1, 1)
            dense_out(0, 1)
            for u in range(2):
                transposed_lo(xaT_lo, xaT_hi, 2, 0, u)
            split_chunk(0, 2)
            split_chunk(0, 3)
            step(0, first=True)
            with dve.Fori(1, E - 1) as e:
                step(e)
            step(E - 1, ahead=False)


_USED = ["x", "adj", "L0_gnn_W_seq", "L0_gnn_a1", "L0_gnn_a2", "L0_gnn_W_out", "L0_gnn_b_out",
         "L0_ffn_ln_g", "L0_ffn_ln_b", "L0_ffn_attn_w", "L0_ffn_attn_b", "L0_ffn_w1", "L0_ffn_b1",
         "L0_ffn_w2", "L0_ffn_b2", "L0_ffn_next_w", "L0_ffn_next_b"]


def kernel(**inputs):
    import numpy as _np
    import concourse.bacc as _bacc
    from concourse.bass_utils import run_bass_kernel_spmd as _run

    nc = _bacc.Bacc("TRN2", target_bir_lowering=False, num_devices=1)
    arrays, args = {}, []
    for name in _USED:
        a = _np.ascontiguousarray(inputs[name])
        arrays[f"in_{name}"] = a
        args.append(nc.dram_tensor(f"in_{name}", a.shape, mybir.dt.from_np(a.dtype), kind="ExternalInput").ap())
    out = nc.dram_tensor("out_rows", (N, D), F32, kind="ExternalOutput").ap()
    gat_moe_kernel(nc, *args, out)
    r = _run(nc, [arrays], core_ids=[0])
    return r.results[0]["out_rows"]
```
